# Optimizing a Trainium2 kernel written in Bass

```python
import numpy as np
import jax
import jax.numpy as jnp

def _softmax(x, axis=-1):
    return jax.nn.softmax(x, axis=axis)

def _gelu(x):
    return jax.nn.gelu(x, approximate=True)

def _silu(x):
    return jax.nn.silu(x)

def _sigmoid(x):
    return jax.nn.sigmoid(x)

def _layernorm(x, axis=-1, eps=1e-05):
    m = jnp.mean(x, axis=axis, keepdims=True)
    v = jnp.var(x, axis=axis, keepdims=True)
    return (x - m) / jnp.sqrt(v + eps)

def _scatter_add(tgt, idx, src, axis=0):
    return tgt.at[idx].add(src)

def _segment_sum(src, seg, n):
    return jax.ops.segment_sum(src, seg, n)
kernel_name = 'mk_dlrm_tower_d1_rec_r8_b82193'

def setup_inputs(seed: int=0):
    np.random.seed(seed)
    _w = jnp.asarray

    def _rec_inputs():
        import jax
        import jax.numpy as jnp
        _tk = jax.random.key(seed)
        dense_ctx = jax.random.normal(jax.random.fold_in(_tk, 190), (2048, 16), jnp.float32)
        ids = jnp.stack([jax.random.randint(jax.random.fold_in(_tk, 200 + f), (2048,), 0, v, jnp.int32) for f, v in enumerate([1000, 1250, 12500, 125000, 12500, 1000, 1000, 1000, 12500, 125000, 12500, 1250, 1000, 1250, 12500, 1250, 125000, 12500, 1000, 12500, 125000, 12500, 125000, 12500, 12500, 1000])], axis=1)
        tbl_0 = 0.05 * jax.random.normal(jax.random.fold_in(_tk, 500 + 0), (1000, 32), jnp.float32)
        tbl_1 = 0.05 * jax.random.normal(jax.random.fold_in(_tk, 500 + 1), (1250, 32), jnp.float32)
        tbl_2 = 0.05 * jax.random.normal(jax.random.fold_in(_tk, 500 + 2), (12500, 32), jnp.float32)
        tbl_3 = 0.05 * jax.random.normal(jax.random.fold_in(_tk, 500 + 3), (125000, 32), jnp.float32)
        tbl_4 = 0.05 * jax.random.normal(jax.random.fold_in(_tk, 500 + 4), (12500, 32), jnp.float32)
        tbl_5 = 0.05 * jax.random.normal(jax.random.fold_in(_tk, 500 + 5), (1000, 32), jnp.float32)
        tbl_6 = 0.05 * jax.random.normal(jax.random.fold_in(_tk, 500 + 6), (1000, 32), jnp.float32)
        tbl_7 = 0.05 * jax.random.normal(jax.random.fold_in(_tk, 500 + 7), (1000, 32), jnp.float32)
        tbl_8 = 0.05 * jax.random.normal(jax.random.fold_in(_tk, 500 + 8), (12500, 32), jnp.float32)
        tbl_9 = 0.05 * jax.random.normal(jax.random.fold_in(_tk, 500 + 9), (125000, 32), jnp.float32)
        tbl_10 = 0.05 * jax.random.normal(jax.random.fold_in(_tk, 500 + 10), (12500, 32), jnp.float32)
        tbl_11 = 0.05 * jax.random.normal(jax.random.fold_in(_tk, 500 + 11), (1250, 32), jnp.float32)
        tbl_12 = 0.05 * jax.random.normal(jax.random.fold_in(_tk, 500 + 12), (1000, 32), jnp.float32)
        tbl_13 = 0.05 * jax.random.normal(jax.random.fold_in(_tk, 500 + 13), (1250, 32), jnp.float32)
        tbl_14 = 0.05 * jax.random.normal(jax.random.fold_in(_tk, 500 + 14), (12500, 32), jnp.float32)
        tbl_15 = 0.05 * jax.random.normal(jax.random.fold_in(_tk, 500 + 15), (1250, 32), jnp.float32)
        tbl_16 = 0.05 * jax.random.normal(jax.random.fold_in(_tk, 500 + 16), (125000, 32), jnp.float32)
        tbl_17 = 0.05 * jax.random.normal(jax.random.fold_in(_tk, 500 + 17), (12500, 32), jnp.float32)
        tbl_18 = 0.05 * jax.random.normal(jax.random.fold_in(_tk, 500 + 18), (1000, 32), jnp.float32)
        tbl_19 = 0.05 * jax.random.normal(jax.random.fold_in(_tk, 500 + 19), (12500, 32), jnp.float32)
        tbl_20 = 0.05 * jax.random.normal(jax.random.fold_in(_tk, 500 + 20), (125000, 32), jnp.float32)
        tbl_21 = 0.05 * jax.random.normal(jax.random.fold_in(_tk, 500 + 21), (12500, 32), jnp.float32)
        tbl_22 = 0.05 * jax.random.normal(jax.random.fold_in(_tk, 500 + 22), (125000, 32), jnp.float32)
        tbl_23 = 0.05 * jax.random.normal(jax.random.fold_in(_tk, 500 + 23), (12500, 32), jnp.float32)
        tbl_24 = 0.05 * jax.random.normal(jax.random.fold_in(_tk, 500 + 24), (12500, 32), jnp.float32)
        tbl_25 = 0.05 * jax.random.normal(jax.random.fold_in(_tk, 500 + 25), (1000, 32), jnp.float32)
        _rk = jax.random.fold_in(_tk, 7)
        W_top1 = 0.0606339 * jax.random.normal(jax.random.fold_in(_tk, 801), (272, 512), jnp.float32)
        W_top2 = 0.0441942 * jax.random.normal(jax.random.fold_in(_tk, 802), (512, 256), jnp.float32)
        W_top3 = 0.0625 * jax.random.normal(jax.random.fold_in(_tk, 803), (256, 1), jnp.float32)
        b_top1 = jnp.zeros((512,), jnp.float32)
        b_top2 = jnp.zeros((256,), jnp.float32)
        return (dense_ctx, ids, tbl_0, tbl_1, tbl_2, tbl_3, tbl_4, tbl_5, tbl_6, tbl_7, tbl_8, tbl_9, tbl_10, tbl_11, tbl_12, tbl_13, tbl_14, tbl_15, tbl_16, tbl_17, tbl_18, tbl_19, tbl_20, tbl_21, tbl_22, tbl_23, tbl_24, tbl_25, W_top1, b_top1, W_top2, b_top2, W_top3)
    dense_ctx, ids, tbl_0, tbl_1, tbl_2, tbl_3, tbl_4, tbl_5, tbl_6, tbl_7, tbl_8, tbl_9, tbl_10, tbl_11, tbl_12, tbl_13, tbl_14, tbl_15, tbl_16, tbl_17, tbl_18, tbl_19, tbl_20, tbl_21, tbl_22, tbl_23, tbl_24, tbl_25, W_top1, b_top1, W_top2, b_top2, W_top3 = _rec_inputs()

    def _L0_rec_setup():
        import jax, jax.numpy as jnp
        import numpy as np
        M_FIELDS = 26
        H1 = 128
        H2 = 128
        BATCH = 256
        EMB_K = 32

        def _cin_layer(x_prev, x0, W, b):
            return jnp.einsum('bik,bjk,hij->bhk', x_prev, x0, W) + b[None, :, None]
        key = jax.random.key(seed)
        k0, k1, k2, k3, k4 = jax.random.split(key, 5)
        inputs = jax.random.normal(k0, (BATCH, M_FIELDS, EMB_K), dtype=jnp.float32)
        W1 = jax.random.normal(k1, (H1, M_FIELDS, M_FIELDS), dtype=jnp.float32) * 0.05
        b1 = jax.random.normal(k2, (H1,), dtype=jnp.float32) * 0.05
        W2 = jax.random.normal(k3, (H2, H1, M_FIELDS), dtype=jnp.float32) * 0.05
        b2 = jax.random.normal(k4, (H2,), dtype=jnp.float32) * 0.05
        return {'inputs': inputs, 'W1': W1, 'b1': b1, 'W2': W2, 'b2': b2}
    _L0_rec_all = _L0_rec_setup()
    _L0_rec_in = {k: v for k, v in _L0_rec_all.items() if k in ('W1', 'b1', 'W2', 'b2')}
    del _L0_rec_all
    return {'dense_ctx': dense_ctx, 'ids': ids, 'tbl_0': tbl_0, 'tbl_1': tbl_1, 'tbl_2': tbl_2, 'tbl_3': tbl_3, 'tbl_4': tbl_4, 'tbl_5': tbl_5, 'tbl_6': tbl_6, 'tbl_7': tbl_7, 'tbl_8': tbl_8, 'tbl_9': tbl_9, 'tbl_10': tbl_10, 'tbl_11': tbl_11, 'tbl_12': tbl_12, 'tbl_13': tbl_13, 'tbl_14': tbl_14, 'tbl_15': tbl_15, 'tbl_16': tbl_16, 'tbl_17': tbl_17, 'tbl_18': tbl_18, 'tbl_19': tbl_19, 'tbl_20': tbl_20, 'tbl_21': tbl_21, 'tbl_22': tbl_22, 'tbl_23': tbl_23, 'tbl_24': tbl_24, 'tbl_25': tbl_25, 'W_top1': W_top1, 'b_top1': b_top1, 'W_top2': W_top2, 'b_top2': b_top2, 'W_top3': W_top3, 'L0_rec_W1': _L0_rec_in['W1'], 'L0_rec_b1': _L0_rec_in['b1'], 'L0_rec_W2': _L0_rec_in['W2'], 'L0_rec_b2': _L0_rec_in['b2']}

def reference(dense_ctx, ids, tbl_0, tbl_1, tbl_2, tbl_3, tbl_4, tbl_5, tbl_6, tbl_7, tbl_8, tbl_9, tbl_10, tbl_11, tbl_12, tbl_13, tbl_14, tbl_15, tbl_16, tbl_17, tbl_18, tbl_19, tbl_20, tbl_21, tbl_22, tbl_23, tbl_24, tbl_25, W_top1, b_top1, W_top2, b_top2, W_top3, L0_rec_W1, L0_rec_b1, L0_rec_W2, L0_rec_b2):
    import jax
    import jax.numpy as jnp

    def _L0_rec_ref(inputs, W1, b1, W2, b2):
        import jax, jax.numpy as jnp
        import numpy as np
        M_FIELDS = 26
        H1 = 128
        H2 = 128
        BATCH = 256
        EMB_K = 32

        def _cin_layer(x_prev, x0, W, b):
            return jnp.einsum('bik,bjk,hij->bhk', x_prev, x0, W) + b[None, :, None]
        x1 = _cin_layer(inputs, inputs, W1, b1)
        x2 = _cin_layer(x1, inputs, W2, b2)
        res = jnp.concatenate([x1, x2], axis=1)
        return jnp.sum(res, axis=-1)
    e = jnp.stack([tbl_0[ids[:, 0]], tbl_1[ids[:, 1]], tbl_2[ids[:, 2]], tbl_3[ids[:, 3]], tbl_4[ids[:, 4]], tbl_5[ids[:, 5]], tbl_6[ids[:, 6]], tbl_7[ids[:, 7]], tbl_8[ids[:, 8]], tbl_9[ids[:, 9]], tbl_10[ids[:, 10]], tbl_11[ids[:, 11]], tbl_12[ids[:, 12]], tbl_13[ids[:, 13]], tbl_14[ids[:, 14]], tbl_15[ids[:, 15]], tbl_16[ids[:, 16]], tbl_17[ids[:, 17]], tbl_18[ids[:, 18]], tbl_19[ids[:, 19]], tbl_20[ids[:, 20]], tbl_21[ids[:, 21]], tbl_22[ids[:, 22]], tbl_23[ids[:, 23]], tbl_24[ids[:, 24]], tbl_25[ids[:, 25]]], axis=1)
    z = _L0_rec_ref(e, L0_rec_W1, L0_rec_b1, L0_rec_W2, L0_rec_b2)
    z = z.reshape(z.shape[0], -1)
    h = jnp.concatenate([z, dense_ctx], axis=1)
    h = jnp.maximum(h @ W_top1 + b_top1, 0.0)
    h = jnp.maximum(h @ W_top2 + b_top2, 0.0)
    y = h @ W_top3
    return y

_drawn_inputs = setup_inputs


def setup_inputs(seed=0):
    import zlib

    import numpy as np

    out = dict(_drawn_inputs(seed))
    spreads = {'b_top1': (0.0, 2.0), 'b_top2': (0.0, 0.8)}
    factors = {'tbl_0': 8.0,
     'tbl_1': 8.0,
     'tbl_2': 8.0,
     'tbl_3': 8.0,
     'tbl_4': 8.0,
     'tbl_5': 8.0,
     'tbl_6': 8.0,
     'tbl_7': 8.0,
     'tbl_8': 8.0,
     'tbl_9': 8.0,
     'tbl_10': 8.0,
     'tbl_11': 8.0,
     'tbl_12': 8.0,
     'tbl_13': 8.0,
     'tbl_14': 8.0,
     'tbl_15': 8.0,
     'tbl_16': 8.0,
     'tbl_17': 8.0,
     'tbl_18': 8.0,
     'tbl_19': 8.0,
     'tbl_20': 8.0,
     'tbl_21': 7.665,
     'tbl_22': 8.0,
     'tbl_23': 8.0,
     'tbl_24': 8.0,
     'tbl_25': 8.0,
     'L0_rec_W1': 8.0,
     'L0_rec_W2': 4.12,
     'dense_ctx': 5.868}
    for name, (base, spread) in spreads.items():
        noise = np.random.default_rng([zlib.crc32(name.encode()), seed]).standard_normal(out[name].shape)
        drawn = base * np.exp(spread * noise) if base else spread * noise
        out[name] = jnp.asarray(drawn.astype(out[name].dtype))
    for name, factor in factors.items():
        out[name] = (out[name] * factor).astype(out[name].dtype)
    return out
```

```python
from contextlib import ExitStack

import concourse.bass as bass
from concourse import mybir

F32 = mybir.dt.float32
I32 = mybir.dt.int32
ALU = mybir.AluOpType
ACT = mybir.ActivationFunctionType

B = 2048
NF = 26
K = 32
H = 128
DN = 16
M1, M2 = 512, 256

NS, ND, NE = 14, 6, 6
S0, D0, E0 = 0, NS, NS + ND
NC = ND + NE


def tri(n):
    return n * (n + 1) // 2


SS0 = 0
DD0 = SS0 + tri(NS)
ONE0 = DD0 + tri(ND)
R0 = ONE0 + 1
SE0 = 0
EE0 = SE0 + NS * NE
XS0 = EE0 + tri(NE)
XE0 = XS0 + NS
R1 = XE0 + NE
C0, C1 = NF + 1, NC + 1
NCOL = C0 + C1
ZD = NCOL
NT = NCOL + ND

P = 128
U = P // K
TILE = 128
G = TILE // U
HG = G // 2
QG = HG // 2
PAIR = 2 * TILE
NPAIR = B // PAIR
BANK = 512

XS, XD = 0, NS + NS // 2 - 1
XE = XD + ND + ND // 2 - 1
SLOTS = XE + NE + NE // 2 - 1

VL = NF * NF + 2


def cyclic_parts(n):
    for d in range(n // 2 + 1):
        last = n // 2 if 2 * d == n else n
        unwrapped = min(n - d, last)
        yield d * n, 0, d, unwrapped, d
        if last > unwrapped:
            yield d * n + unwrapped, unwrapped, 0, last - unwrapped, d


def view(tensor, p0, p1, offset, dims):
    base = tensor[p0:p1, offset:offset + 1]
    return bass.AP(base.tensor, base.offset, [list(base.ap[0])] + [list(d) for d in dims])


def build(nc, t):
    with ExitStack() as ctx:
        def sb(name, shape, dt=F32):
            return ctx.enter_context(nc.sbuf_tensor(name, shape, dt))

        def pb(name, n):
            return ctx.enter_context(nc.psum_tensor(name, [P, n * BANK], F32))

        def sem(name):
            return ctx.enter_context(nc.semaphore(name))

        NSUM = (NF + NC + 2) * PAIR
        NPROD = HG * 2 * P
        region_a = sb("region_a", [P, max((NF + 1) * VL, NSUM + 2 * NPROD)])
        V = region_a
        W1S = NF * VL
        SUMS = 0
        PROD = [NSUM, NSUM + NPROD]
        NDIAG = HG * U * C0
        region_b = sb("region_b", [P, max(NT * P, 2 * NDIAG + (2 + 4 + 2) * PAIR)])
        WROW = region_b
        DIAG = [0, NDIAG]
        z_sb = region_b[:, 2 * NDIAG:2 * NDIAG + 2 * PAIR]
        h1_sb = region_b[:, 2 * NDIAG + 2 * PAIR:2 * NDIAG + 6 * PAIR]
        h2_sb = region_b[:, 2 * NDIAG + 6 * PAIR:2 * NDIAG + 8 * PAIR]
        w2_sb = sb("w2_sb", [P, NF * H])
        w1_raw = sb("w1_raw", [P, NF * NF])
        weights = sb("weights", [P, NT * H])
        index = [sb(f"index{n}", [P, NF], I32) for n in range(2)]
        rows = [sb(f"rows{n}", [P, NF * K]) for n in range(2)]
        x = [sb(f"x{n}", [P, SLOTS * G]) for n in range(2)]
        wt1 = sb("wt1", [P, 2 * M1])
        wt1d = sb("wt1d", [DN, M1])
        wt2 = sb("wt2", [P, 4 * M2])
        wt3 = sb("wt3", [P, 2])
        bt1 = sb("bt1", [P, 4])
        bt2 = sb("bt2", [P, 2])
        b2 = sb("b2", [P, 1])
        b2k = sb("b2k", [P, 1])
        ident = sb("ident", [P, P])
        turn = sb("turn", [1, 2])
        side = sb("side", [64, B])
        YP = 32

        sum_ps = [pb(f"sum_ps{n}", 3) for n in range(2)]
        gen = [pb(f"gen{n}", 1) for n in range(2)]

        index_in = [sem(f"index_in{n}") for n in range(2)]
        gathered = [sem(f"gathered{n}") for n in range(2)]
        w1_in, w2_in, ident_in, top_in = sem("w1_in"), sem("w2_in"), sem("ident_in"), sem("top_in")
        turns = sem("turns")
        ident0 = sem("ident0")
        w1_sum, w1_ready = sem("w1_sum"), sem("w1_ready")
        v_summed, v_saved = sem("v_summed"), sem("v_saved")
        wrow_first, wrow_ready = sem("wrow_first"), sem("wrow_ready")
        w_turned, w_saved = sem("w_turned"), sem("w_saved")
        diag_zero, consts = sem("diag_zero"), sem("consts")
        x_ready = sem("x_ready")
        prod_ready = sem("prod_ready")
        diag_ready = sem("diag_ready")
        summed = sem("summed")
        sums_saved = sem("sums_saved")
        z_summed, z_saved = sem("z_summed"), sem("z_saved")
        h1_summed, h1_saved = sem("h1_summed"), sem("h1_saved")
        h2_summed, h2_saved = sem("h2_summed"), sem("h2_saved")
        y_summed, y_saved, y_out = sem("y_summed"), sem("y_saved"), sem("y_out")

        GATHERED = 16 * NF
        TOP_IN = 16 * 8

        block = ctx.enter_context(nc.Block())

        @block.sync
        def _(sp):
            for n in range(2):
                sp.dma_start(index[n][:, :], t["ids"][n * TILE:(n + 1) * TILE, :]).then_inc(index_in[n], 16)
            sp.dma_start(w1_raw[:, :], t["L0_rec_W1"].rearrange("h i j -> h (i j)")).then_inc(w1_in, 16)
            sp.dma_start(view(region_a, 0, P, W1S + NF * NF, [[1, 1]]), t["L0_rec_b1"]).then_inc(w1_in, 16)
            sp.dma_start(w2_sb[:, :], t["L0_rec_W2"].rearrange("i l h -> i (l h)")).then_inc(w2_in, 16)
            sp.dma_start(wt1[:, :], t["W_top1"][0:2 * H, :].rearrange("(c p) n -> p c n", p=P)).then_inc(top_in, 16)
            sp.dma_start(wt1d[:, :], t["W_top1"][2 * H:2 * H + DN, :]).then_inc(top_in, 16)
            sp.dma_start(wt2[:, :], t["W_top2"].rearrange("(c p) n -> p c n", p=P)).then_inc(top_in, 16)
            sp.dma_start(wt3[:, :], t["W_top3"]).then_inc(top_in, 16)
            sp.dma_start(bt1[:, :], t["b_top1"]).then_inc(top_in, 16)
            sp.dma_start(bt2[:, :], t["b_top2"]).then_inc(top_in, 16)
            sp.dma_start(b2[:, :], t["L0_rec_b2"]).then_inc(top_in, 16)
            sp.dma_start(side[0:DN, :], t["dense_ctx"]).then_inc(top_in, 16)
            with sp.Fori(1, NPAIR) as j:
                for n in range(2):
                    sp.wait_ge(gathered[n], GATHERED * j)
                    sp.dma_start(index[n][:, :], t["ids"][bass.ds(j * PAIR + n * TILE, TILE), :]).then_inc(index_in[n], 16)
            sp.wait_ge(y_saved, NPAIR)
            sp.dma_start(t["out"], side[YP:YP + 1, :]).then_inc(y_out, 16)
            sp.wait_ge(y_out, 16)

        @block.gpsimd
        def _(pool):
            def gather(j, n, first):
                pool.wait_ge(index_in[n], 16 * (j + 1))
                if not first:
                    pool.wait_ge(x_ready, 2 * j + n - 1)
                    pool.wait_ge(turns, 2 * j + n - 1)
                    nc.gpsimd.tensor_tensor(turn[:, 1:2], turn[:, 0:1], turn[:, 0:1], ALU.add).then_inc(turns, 1)
                for f in range(NF):
                    pool.indirect_dma_start(
                        out=rows[n][:, f * K:(f + 1) * K], out_offset=None, in_=t[f"tbl_{f}"],
                        in_offset=bass.IndirectOffsetOnAxis(ap=index[n][:, f:f + 1], axis=0),
                    ).then_inc(gathered[n], 16)

            gather(0, 0, True)
            nc.gpsimd.memset(turn[:, :], 0.0).then_inc(turns, 1)
            nc.gpsimd.memset(ident[:, :], 0.0).then_inc(ident0, 1)
            pool.wait_ge(ident0, 1)
            nc.gpsimd.affine_select(out=ident[:, :], in_=ident[:, :], compare_op=ALU.not_equal, fill=1.0, base=0,
                                    pattern=[[-1, P]], channel_multiplier=1).then_inc(ident_in, 1)
            gather(0, 1, True)
            with pool.Fori(1, NPAIR) as j:
                for n in range(2):
                    gather(j, n, False)

        @block.vector
        def _(dve):
            dve.wait_ge(w1_in, 32)
            nc.vector.tensor_tensor(view(V, 0, P, W1S, [[NF, NF], [1, NF]]), view(w1_raw, 0, P, 0, [[NF, NF], [1, NF]]),
                                    view(w1_raw, 0, P, 0, [[1, NF], [NF, NF]]), ALU.add).then_inc(w1_sum, 1)
            nc.vector.memset(view(V, 0, P, W1S + VL - 1, [[1, 1]]), 0.0)
            nc.vector.memset(WROW[:, NCOL * P:NT * P], 0.0)
            nc.vector.memset(view(WROW, 0, P, C0 * P, [[P, C1], [1, P]]), 0.0)
            nc.vector.memset(view(WROW, 0, P, ONE0, [[P, C0], [1, P - ONE0]]), 0.0).then_inc(w1_sum, 1)
            dve.wait_ge(w1_sum, 2)
            diagonal = view(V, 0, P, W1S, [[NF + 1, NF]])
            nc.vector.tensor_scalar(diagonal, diagonal, 0.5, None, ALU.mult).then_inc(w1_ready, 1)
            dve.wait_ge(w1_ready, 1)
            dve.wait_ge(v_saved, NF)

            def v(l, i, j, dims):
                return view(V, 0, P, l * VL + i * NF + j, [[a * VL + b * NF + c, n] for a, b, c, n in dims])

            def w(col, row, dims):
                return view(WROW, 0, P, col * P + row, [[a * P + b, n] for a, b, n in dims])

            add, copy = nc.vector.tensor_tensor, nc.vector.tensor_copy

            def columns(lo, hi, first_col, row0, n, f0, symmetric):
                for r, i, j, count, d in cyclic_parts(n):
                    out = w(first_col, row0 + r, [(1, 0, hi - lo), (0, 1, count)])
                    direct = v(lo, f0 + i, f0 + j, [(1, 0, 0, hi - lo), (0, 1, 1, count)])
                    if symmetric:
                        add(out, direct, v(f0 + j, f0 + i, lo, [(0, 0, 1, hi - lo), (1, 1, 0, count)]), ALU.add)
                    else:
                        copy(out, direct)

            def columns_rest(lo, hi, first_col, row0, n, f0):
                for r, i, j, count, d in cyclic_parts(n):
                    if d:
                        out = w(first_col, row0 + r, [(1, 0, hi - lo), (0, 1, count)])
                        add(out, out, v(f0 + i, f0 + j, lo, [(0, 0, 1, hi - lo), (1, 1, 0, count)]), ALU.add)

            columns(S0, D0, S0, SS0, NS, S0, False)
            columns(D0, NF, D0, SS0, NS, S0, True)
            columns(NF, NF + 1, NF, SS0, NS, S0, False)
            columns(S0, D0, S0, DD0, ND, D0, True)
            columns(D0, E0, D0, DD0, ND, D0, False)
            columns(E0, NF, E0, DD0, ND, D0, True)
            columns(NF, NF + 1, NF, DD0, ND, D0, False)
            copy(w(0, ONE0, [(1, 0, C0)]), v(0, NF, 0, [(1, 0, 0, C0)]))
            add(w(C0, SE0, [(1, 0, ND), (0, NS, NE), (0, 1, NS)]),
                v(D0, S0, E0, [(1, 0, 0, ND), (0, 0, 1, NE), (0, 1, 0, NS)]),
                v(E0, S0, D0, [(0, 0, 1, ND), (1, 0, 0, NE), (0, 1, 0, NS)]), ALU.add)
            copy(w(C0 + ND, SE0, [(1, 0, NE + 1), (0, NS, NE), (0, 1, NS)]),
                 v(E0, S0, E0, [(1, 0, 0, NE + 1), (0, 0, 1, NE), (0, 1, 0, NS)]))
            columns(D0, E0, C0, EE0, NE, E0, True)
            columns(E0, NF + 1, C0 + ND, EE0, NE, E0, False)
            copy(w(ZD, XS0, [(1, 0, ND), (0, 1, NS)]), v(NF, S0, D0, [(0, 0, 1, ND), (0, 1, 0, NS)]))
            copy(w(ZD, XE0, [(1, 0, ND), (0, 1, NE)]), v(NF, E0, D0, [(0, 0, 1, ND), (0, 1, 0, NE)])).then_inc(wrow_first, 1)
            dve.wait_ge(wrow_first, 1)
            columns_rest(D0, NF, D0, SS0, NS, S0)
            columns_rest(S0, D0, S0, DD0, ND, D0)
            columns_rest(E0, NF, E0, DD0, ND, D0)
            columns_rest(D0, E0, C0, EE0, NE, E0)
            for e in range(NE):
                out = w(C0 + ND + e, SE0 + e * NS, [(1, 0, NE - e), (0, 1, NS)])
                add(out, out, v(S0, E0 + e, E0 + e, [(0, 0, 1, NE - e), (1, 0, 0, NS)]), ALU.add)
            out = w(C0, SE0, [(1, 0, ND), (0, NS, NE), (0, 1, NS)])
            add(out, out, v(S0, E0, D0, [(0, 0, 1, ND), (0, 1, 0, NE), (1, 0, 0, NS)]), ALU.add).then_inc(wrow_ready, 1)
            dve.wait_ge(wrow_ready, 1)
            for n in range(2):
                nc.vector.memset(view(region_a, 0, P, PROD[n] + ONE0, [[2 * P, HG]]), 1.0)
            dve.wait_ge(top_in, TOP_IN)
            nc.vector.tensor_scalar(b2k[:, :], b2[:, :], float(K), None, ALU.mult)
            dve.wait_ge(w_turned, (NT + 3) // 4)
            nc.vector.memset(region_b[:, 0:2 * NDIAG], 0.0).then_inc(diag_zero, 1)
            dve.wait_ge(diag_zero, 1)
            for u in range(U):
                for n in range(2):
                    last = nc.vector.memset(view(region_b, u * K, (u + 1) * K, DIAG[n] + u * C0 + NF, [[U * C0, HG]]), 1.0)
            last.then_inc(consts, 1)

            mul = nc.vector.tensor_tensor

            def products(n, h):
                xt, at = x[n], h * HG

                def p(row, dims):
                    return view(region_a, 0, P, PROD[h] + row, dims + [[2 * P, HG]])

                def xs(slot, dims):
                    return view(xt, 0, P, slot * G + at, dims + [[1, HG]])

                for first_row, slot, m in ((SS0, XS, NS), (DD0, XD, ND), (P + EE0, XE, NE)):
                    mul(p(first_row, [[m, m // 2], [1, m]]), xs(slot, [[0, m // 2], [G, m]]),
                        xs(slot, [[G, m // 2], [G, m]]), ALU.mult)
                    mul(p(first_row + m * (m // 2), [[1, m // 2]]), xs(slot, [[G, m // 2]]),
                        xs(slot + m // 2, [[G, m // 2]]), ALU.mult)
                mul(p(P + SE0, [[NS, NE], [1, NS]]), xs(XE, [[G, NE], [0, NS]]), xs(XS, [[0, NE], [G, NS]]), ALU.mult)
                copy(p(P + XS0, [[1, NS]]), xs(XS, [[G, NS]]))
                copy(p(P + XE0, [[1, NE]]), xs(XE, [[G, NE]])).then_inc(prod_ready, 1)

            def tile(j, n, first):
                dve.wait_ge(gathered[n], GATHERED * (j + 1))
                if not first:
                    dve.wait_ge(diag_ready, 4 * j + 2 * n - 2)
                for slot, f, m in ((XS, S0, NS), (XS + NS, S0, NS // 2 - 1), (XD, D0, ND), (XD + ND, D0, ND // 2 - 1),
                                   (XE, E0, NE), (XE + NE, E0, NE // 2 - 1)):
                    last = nc.vector.transpose(x[n][:, slot * G:(slot + m) * G], rows[n][:, f * K:(f + m) * K])
                last.then_inc(x_ready, 1)
                dve.wait_ge(x_ready, 2 * j + n + 1)
                for h in range(2):
                    if not (first and n == 0):
                        dve.wait_ge(summed, 8 * j + 4 * n + 2 * h - 2)
                    products(n, h)

            for n in range(2):
                tile(0, n, True)
            with dve.Fori(1, NPAIR) as j:
                for n in range(2):
                    tile(j, n, False)

        @block.scalar
        def _(act):
            for l in range(NF):
                act.wait_ge(v_summed, l + 1)
                nc.scalar.copy(view(V, 0, P, l * VL, [[VL // 2, 2], [1, VL // 2]]),
                               view(sum_ps[l % 2], 0, P, 0, [[BANK, 2], [1, VL // 2]])).then_inc(v_saved, 1)
            for q in range((NT + 3) // 4):
                m = min(4, NT - 4 * q)
                act.wait_ge(w_turned, q + 1)
                nc.scalar.copy(weights[:, 4 * q * H:(4 * q + m) * H], gen[q % 2][:, 0:m * H]).then_inc(w_saved, 1)
            act.wait_ge(consts, 1)
            act.wait_ge(top_in, TOP_IN)

            def diagonal(n, h):
                for u in range(U):
                    for slot, a, m in ((XS, S0, NS), (XD, D0, ND), (XE, E0, NE)):
                        last = nc.scalar.copy(
                            view(region_b, u * K, (u + 1) * K, DIAG[h] + u * C0 + a, [[1, m], [U * C0, HG]]),
                            view(x[n], u * K, (u + 1) * K, slot * G + h * HG, [[G, m], [1, HG]]))
                last.then_inc(diag_ready, 1)

            def save_sums(n, q):
                ps, at = sum_ps[q % 2], SUMS + n * TILE + q * QG * U
                nc.scalar.copy(view(region_a, 0, R0, at, [[PAIR, C0], [QG // 2 * U, 2], [1, QG // 2 * U]]),
                               view(ps, 0, R0, 0, [[1, C0], [BANK, 2], [C0, QG // 2 * U]]))
                nc.scalar.copy(view(region_a, 0, R1, at + C0 * PAIR, [[PAIR, C1], [1, QG * U]]),
                               view(ps, 0, R1, 2 * BANK, [[1, C1], [C1, QG * U]])).then_inc(sums_saved, 1)

            def pair(j, first):
                for n in range(2):
                    act.wait_ge(x_ready, 2 * j + n + 1)
                    for h in range(2):
                        if not (first and n == 0):
                            act.wait_ge(summed, 8 * j + 4 * n + 2 * h - 2)
                        diagonal(n, h)
                    for q in range(4):
                        act.wait_ge(summed, 8 * j + 4 * n + q + 1)
                        if not first and n == 0 and q == 0:
                            act.wait_ge(z_summed, 2 * j)
                        save_sums(n, q)
                act.wait_ge(z_summed, 2 * j + 2)
                for i in range(2):
                    nc.scalar.activation(z_sb[:, i * PAIR:(i + 1) * PAIR], gen[0][:, i * PAIR:(i + 1) * PAIR],
                                         ACT.Identity, bias=b2k[:, :] if i else 0.0).then_inc(z_saved, 1)
                for m in range(4):
                    if m % 2 == 0:
                        act.wait_ge(h1_summed, 4 * j + m + 2)
                    nc.scalar.activation(h1_sb[:, m * PAIR:(m + 1) * PAIR],
                                         gen[1 - m // 2][:, m % 2 * PAIR:(m % 2 + 1) * PAIR], ACT.Relu,
                                         bias=bt1[:, m:m + 1]).then_inc(h1_saved, 1)
                act.wait_ge(h2_summed, 2 * j + 2)
                for m in range(2):
                    nc.scalar.activation(h2_sb[:, m * PAIR:(m + 1) * PAIR], gen[1][:, m * PAIR:(m + 1) * PAIR], ACT.Relu,
                                         bias=bt2[:, m:m + 1]).then_inc(h2_saved, 1)
                act.wait_ge(y_summed, j + 1)
                nc.scalar.copy(side[YP:YP + 1, bass.ds(j * PAIR, PAIR)], gen[0][0:1, 0:PAIR]).then_inc(y_saved, 1)

            pair(0, True)
            with act.Fori(1, NPAIR) as j:
                pair(j, False)

        @block.tensor
        def _(pe):
            pe.wait_ge(w2_in, 16)
            pe.wait_ge(w1_ready, 1)
            for l in range(NF):
                if l >= 2:
                    pe.wait_ge(v_saved, l - 1)
                for half in range(2):
                    last = nc.tensor.matmul(sum_ps[l % 2][:, half * BANK:half * BANK + VL // 2], w2_sb[:, l * H:(l + 1) * H],
                                            view(V, 0, P, W1S + half * (VL // 2), [[1, VL // 2]]), start=True, stop=True)
                last.then_inc(v_summed, 1)
            pe.wait_ge(ident_in, 1)
            pe.wait_ge(wrow_ready, 1)
            for q in range((NT + 3) // 4):
                if q >= 2:
                    pe.wait_ge(w_saved, q - 1)
                for c in range(4 * q, min(4 * q + 4, NT)):
                    last = nc.tensor.transpose(gen[q % 2][:, c % 4 * H:(c % 4 + 1) * H], WROW[:, c * P:(c + 1) * P], ident[:, :])
                last.then_inc(w_turned, 1)

            def sums(n, h, q):
                ps = sum_ps[q % 2]
                for g in range(QG):
                    gh = (q % 2) * QG + g
                    prod = PROD[h] + gh * 2 * P
                    diag = DIAG[h] + gh * U * C0
                    o = (g // (QG // 2)) * BANK + g % (QG // 2) * U * C0
                    nc.tensor.matmul(ps[0:R0, o:o + U * C0], region_a[:, prod:prod + R0],
                                     region_b[:, diag:diag + U * C0], start=True, stop=True)
                    o = 2 * BANK + g * U * C1
                    last = nc.tensor.matmul(view(ps, 0, R1, o, [[C1, U], [1, C1]]), region_a[:, prod + P:prod + P + R1],
                                            view(region_b, 0, P, diag + D0, [[C0, U], [1, C1]]), start=True, stop=True)
                last.then_inc(summed, 1)

            def weight(block_rows, c):
                return weights[0:block_rows, c * H:(c + 1) * H]

            def saved(block_rows, c):
                return view(region_a, 0, block_rows, SUMS + c * PAIR, [[1, PAIR]])

            def pair(j, first):
                for n in range(2):
                    for q in range(4):
                        if not (first and n == 0 and q < 2):
                            pe.wait_ge(sums_saved, 8 * j + 4 * n + q - 1)
                        if q % 2 == 0:
                            pe.wait_ge(prod_ready, 4 * j + 2 * n + q // 2 + 1)
                            pe.wait_ge(diag_ready, 4 * j + 2 * n + q // 2 + 1)
                        sums(n, q // 2, q)
                if not first:
                    pe.wait_ge(y_saved, j)
                pe.wait_ge(sums_saved, 8 * j + 8)
                z1 = [(R0, NF, NF), (R1, C0 + NC, C0 + NC)] + [(R1, ZD + d, C0 + d) for d in range(ND)]
                z2 = [(R0, a, a) for a in range(NF)] + [(R1, C0 + a, C0 + a) for a in range(NC)]
                for i, terms in enumerate((z1, z2)):
                    for m, (r, wc, sc) in enumerate(terms):
                        last = nc.tensor.matmul(gen[0][:, i * PAIR:(i + 1) * PAIR], weight(r, wc), saved(r, sc),
                                                start=m == 0, stop=m == len(terms) - 1)
                    last.then_inc(z_summed, 1)
                pe.wait_ge(z_saved, 2 * j + 2)
                for m in range(4):
                    out = gen[1 - m // 2][:, m % 2 * PAIR:(m % 2 + 1) * PAIR]
                    for c in range(2):
                        nc.tensor.matmul(out, wt1[:, c * M1 + m * P:c * M1 + (m + 1) * P], z_sb[:, c * PAIR:(c + 1) * PAIR],
                                         start=c == 0, stop=False)
                    nc.tensor.matmul(out, wt1d[:, m * P:(m + 1) * P], side[0:DN, bass.ds(j * PAIR, PAIR)],
                                     start=False, stop=True).then_inc(h1_summed, 1)
                pe.wait_ge(h1_saved, 4 * j + 4)
                for m in range(2):
                    for c in range(4):
                        last = nc.tensor.matmul(gen[1][:, m * PAIR:(m + 1) * PAIR], wt2[:, c * M2 + m * P:c * M2 + (m + 1) * P],
                                                h1_sb[:, c * PAIR:(c + 1) * PAIR], start=c == 0, stop=c == 3)
                    last.then_inc(h2_summed, 1)
                pe.wait_ge(h2_saved, 2 * j + 2)
                for c in range(2):
                    last = nc.tensor.matmul(gen[0][0:1, 0:PAIR], wt3[:, c:c + 1], h2_sb[:, c * PAIR:(c + 1) * PAIR],
                                            start=c == 0, stop=c == 1)
                last.then_inc(y_summed, 1)

            pe.wait_ge(w_saved, (NT + 3) // 4)
            pe.wait_ge(top_in, TOP_IN)
            pair(0, True)
            with pe.Fori(1, NPAIR) as j:
                pair(j, False)


def kernel(**inputs):
    import numpy as np
    import concourse.bacc as bacc
    from concourse.bass_utils import run_bass_kernel_spmd

    nc = bacc.Bacc("TRN2", target_bir_lowering=False, num_devices=1)
    a = {name: np.asarray(v) for name, v in inputs.items()}
    a["L0_rec_W2"] = a["L0_rec_W2"].transpose(1, 2, 0)
    a["dense_ctx"] = a["dense_ctx"].reshape(B // TILE, U, G, DN).transpose(3, 0, 2, 1).reshape(DN, B)
    a["b_top1"] = a["b_top1"].reshape(M1 // P, P).T
    a["b_top2"] = a["b_top2"].reshape(M2 // P, P).T
    a["W_top3"] = a["W_top3"].reshape(M2 // P, P).T
    a["L0_rec_b1"] = a["L0_rec_b1"].reshape(H, 1)
    a["L0_rec_b2"] = a["L0_rec_b2"].reshape(H, 1)
    arrays, t = {}, {}
    for name, v in a.items():
        arrays[name] = np.ascontiguousarray(v)
        t[name] = nc.dram_tensor(name, v.shape, mybir.dt.from_np(v.dtype), kind="ExternalInput").ap()
    t["out"] = nc.dram_tensor("out", (1, B), F32, kind="ExternalOutput").ap()
    build(nc, t)
    r = run_bass_kernel_spmd(nc, [arrays], core_ids=[0])
    y = r.results[0]["out"]
    return y.reshape(B // TILE, G, U).transpose(0, 2, 1).reshape(B, 1)
```

```python
from contextlib import ExitStack

import concourse.bass as bass
from concourse import mybir

F32 = mybir.dt.float32
I32 = mybir.dt.int32
ALU = mybir.AluOpType
ACT = mybir.ActivationFunctionType

B = 2048
NF = 26
K = 32
H = 128
DN = 16
M1, M2 = 512, 256

NS, ND, NE = 14, 6, 6
S0, D0, E0 = 0, NS, NS + ND
NC = ND + NE


def tri(n):
    return n * (n + 1) // 2


SS0 = 0
DD0 = SS0 + tri(NS)
ONE0 = DD0 + tri(ND)
R0 = ONE0 + 1
SE0 = 0
EE0 = SE0 + NS * NE
XS0 = EE0 + tri(NE)
XE0 = XS0 + NS
R1 = XE0 + NE
C0, C1 = NF + 1, NC + 1
NCOL = C0 + C1
NX = NS + NE
RX = ND * NX
ZX = NCOL
NT = NCOL + 1

P = 128
U = P // K
TILE = 128
G = TILE // U
HG = G // 2
QG = HG // 2
PAIR = 2 * TILE
NPAIR = B // PAIR
BANK = 512

XS, XD = 0, NS + NS // 2 - 1
XE = XD + ND + ND // 2 - 1
SLOTS = XE + NE + NE // 2 - 1

VS, VC = NS * NF, NC * NC
VB = VS + VC
VL = VB + 2


def cyclic_parts(n):
    for d in range(n // 2 + 1):
        last = n // 2 if 2 * d == n else n
        unwrapped = min(n - d, last)
        yield d * n, 0, d, unwrapped, d
        if last > unwrapped:
            yield d * n + unwrapped, unwrapped, 0, last - unwrapped, d


def view(tensor, p0, p1, offset, dims):
    base = tensor[p0:p1, offset:offset + 1]
    return bass.AP(base.tensor, base.offset, [list(base.ap[0])] + [list(d) for d in dims])


def build(nc, t):
    with ExitStack() as ctx:
        def sb(name, shape, dt=F32):
            return ctx.enter_context(nc.sbuf_tensor(name, shape, dt))

        def pb(name, n):
            return ctx.enter_context(nc.psum_tensor(name, [P, n * BANK], F32))

        def sem(name):
            return ctx.enter_context(nc.semaphore(name))

        region_a = sb("region_a", [P, max((NF + 1) * VL, NCOL * PAIR)])
        V = region_a
        W1S = NF * VL
        SUMS = 0
        NPROD = HG * 2 * P
        prod = sb("prod", [P, 2 * NPROD])
        PROD = [0, NPROD]
        w2_sb = prod[:, NPROD:NPROD + NF * H]
        W1_RAW = NPROD + NF * H
        NDIAG = HG * U * C0
        diag = sb("diag", [P, 2 * NDIAG])
        DIAG = [0, NDIAG]
        TOPW = 8 * PAIR
        region_b = sb("region_b", [P, max(NT * P, TOPW + 3 * M1 + 4 * M2)])
        WROW = region_b
        z_sb = region_b[:, 0:2 * PAIR]
        h1_sb = region_b[:, 2 * PAIR:6 * PAIR]
        h2_sb = region_b[:, 6 * PAIR:8 * PAIR]
        wt1 = region_b[:, TOPW:TOPW + 2 * M1]
        wt1d = region_b[0:DN, TOPW + 2 * M1:TOPW + 3 * M1]
        wt2 = region_b[:, TOPW + 3 * M1:TOPW + 3 * M1 + 4 * M2]
        weights = sb("weights", [P, NT * H])
        index = [sb(f"index{n}", [P, NF], I32) for n in range(2)]
        rows = [sb(f"rows{n}", [P, NF * K]) for n in range(2)]
        x = [sb(f"x{n}", [P, SLOTS * G]) for n in range(2)]
        wt3 = sb("wt3", [P, 2])
        bt1 = sb("bt1", [P, 4])
        bt2 = sb("bt2", [P, 2])
        b2 = sb("b2", [P, 1])
        b2k = sb("b2k", [P, 1])
        ident = sb("ident", [P, P])
        turn = sb("turn", [1, 2])
        cross = sb("cross", [RX, PAIR])
        side = sb("side", [64, B])
        YP = 32

        sum_ps = [pb(f"sum_ps{n}", 3) for n in range(2)]
        gen = [pb(f"gen{n}", 1) for n in range(2)]

        index_in = [sem(f"index_in{n}") for n in range(2)]
        gathered = [sem(f"gathered{n}") for n in range(2)]
        w1_in, w2_in, ident_in = sem("w1_in"), sem("w2_in"), sem("ident_in")
        small_in, top_in = sem("small_in"), sem("top_in")
        turns = sem("turns")
        ident0 = sem("ident0")
        w1_sum, w1_ready = sem("w1_sum"), sem("w1_ready")
        v_summed, v_saved = sem("v_summed"), sem("v_saved")
        wrow_first, wrow_ready = sem("wrow_first"), sem("wrow_ready")
        w_turned, w_saved = sem("w_turned"), sem("w_saved")
        diag_zero, diag_set = sem("diag_zero"), sem("diag_set")
        x_ready = sem("x_ready")
        prod_ready = sem("prod_ready")
        diag_ready = sem("diag_ready")
        summed = sem("summed")
        sums_saved = sem("sums_saved")
        sums0_saved = sem("sums0_saved")
        cross_in = sem("cross_in")
        z_summed, z_saved = sem("z_summed"), sem("z_saved")
        h1_summed, h1_saved = sem("h1_summed"), sem("h1_saved")
        h2_summed, h2_saved = sem("h2_summed"), sem("h2_saved")
        y_summed, y_saved, y_out = sem("y_summed"), sem("y_saved"), sem("y_out")

        GATHERED = 16 * NF
        CROSS_IN = 16 * ND
        SMALL_IN = 16 * 5
        TOP_IN = 16 * 3

        NTURN = -(-NT // 4)

        block = ctx.enter_context(nc.Block())

        @block.sync
        def _(sp):
            for n in range(2):
                sp.dma_start(index[n][:, :], t["ids"][n * TILE:(n + 1) * TILE, :]).then_inc(index_in[n], 16)
            sp.dma_start(prod[:, W1_RAW:W1_RAW + NF * NF], t["L0_rec_W1"].rearrange("h i j -> h (i j)")).then_inc(w1_in, 16)
            sp.dma_start(region_a[:, W1S + VB:W1S + VB + 1], t["L0_rec_b1"]).then_inc(w1_in, 16)
            sp.dma_start(w2_sb, t["L0_rec_W2"].rearrange("i l h -> i (l h)")).then_inc(w2_in, 16)
            sp.dma_start(wt3[:, :], t["W_top3"]).then_inc(small_in, 16)
            sp.dma_start(bt1[:, :], t["b_top1"]).then_inc(small_in, 16)
            sp.dma_start(bt2[:, :], t["b_top2"]).then_inc(small_in, 16)
            sp.dma_start(b2[:, :], t["L0_rec_b2"]).then_inc(small_in, 16)
            sp.dma_start(side[0:DN, :], t["dense_ctx"]).then_inc(small_in, 16)
            sp.wait_ge(w_turned, NTURN)
            sp.dma_start(wt1, t["W_top1"][0:2 * H, :].rearrange("(c p) n -> p c n", p=P)).then_inc(top_in, 16)
            sp.dma_start(wt1d, t["W_top1"][2 * H:2 * H + DN, :]).then_inc(top_in, 16)
            sp.dma_start(wt2, t["W_top2"].rearrange("(c p) n -> p c n", p=P)).then_inc(top_in, 16)
            with sp.Fori(1, NPAIR) as j:
                for n in range(2):
                    sp.wait_ge(gathered[n], GATHERED * j)
                    sp.dma_start(index[n][:, :], t["ids"][bass.ds(j * PAIR + n * TILE, TILE), :]).then_inc(index_in[n], 16)
            sp.wait_ge(y_saved, NPAIR)
            sp.dma_start(t["out"], side[YP:YP + 1, :]).then_inc(y_out, 16)
            sp.wait_ge(y_out, 16)

        @block.gpsimd
        def _(pool):
            def gather(j, n, first):
                pool.wait_ge(index_in[n], 16 * (j + 1))
                if not first:
                    pool.wait_ge(x_ready, 2 * j + n - 1)
                    pool.wait_ge(turns, 2 * j + n - 1)
                    nc.gpsimd.tensor_tensor(turn[:, 1:2], turn[:, 0:1], turn[:, 0:1], ALU.add).then_inc(turns, 1)
                for f in range(NF):
                    pool.indirect_dma_start(
                        out=rows[n][:, f * K:(f + 1) * K], out_offset=None, in_=t[f"tbl_{f}"],
                        in_offset=bass.IndirectOffsetOnAxis(ap=index[n][:, f:f + 1], axis=0),
                    ).then_inc(gathered[n], 16)

            gather(0, 0, True)
            nc.gpsimd.memset(turn[:, :], 0.0).then_inc(turns, 1)
            nc.gpsimd.memset(ident[:, :], 0.0).then_inc(ident0, 1)
            pool.wait_ge(ident0, 1)
            nc.gpsimd.affine_select(out=ident[:, :], in_=ident[:, :], compare_op=ALU.not_equal, fill=1.0, base=0,
                                    pattern=[[-1, P]], channel_multiplier=1).then_inc(ident_in, 1)
            gather(0, 1, True)
            with pool.Fori(1, NPAIR) as j:
                for n in range(2):
                    gather(j, n, False)

        @block.vector
        def _(dve):
            add, copy = nc.vector.tensor_tensor, nc.vector.tensor_copy
            nc.vector.memset(diag[:, :], 0.0).then_inc(diag_zero, 1)
            nc.vector.memset(region_a[:, W1S + VB + 1:W1S + VL], 0.0)
            nc.vector.memset(WROW[:, NCOL * P:NT * P], 0.0)
            nc.vector.memset(view(WROW, 0, P, C0 * P, [[P, C1], [1, P]]), 0.0)
            nc.vector.memset(view(WROW, 0, P, ONE0, [[P, C0], [1, P - ONE0]]), 0.0)
            dve.wait_ge(w1_in, 32)
            add(view(V, 0, P, W1S, [[NF, NS], [1, NF]]), view(prod, 0, P, W1_RAW, [[NF, NS], [1, NF]]),
                view(prod, 0, P, W1_RAW, [[1, NS], [NF, NF]]), ALU.add)
            corner = W1_RAW + NS * NF + NS
            add(view(V, 0, P, W1S + VS, [[NC, NC], [1, NC]]), view(prod, 0, P, corner, [[NF, NC], [1, NC]]),
                view(prod, 0, P, corner, [[1, NC], [NF, NC]]), ALU.add).then_inc(w1_sum, 1)
            dve.wait_ge(w1_sum, 1)
            for first, step, n in ((W1S, NF + 1, NS), (W1S + VS, NC + 1, NC)):
                on_diagonal = view(V, 0, P, first, [[step, n]])
                last = nc.vector.tensor_scalar(on_diagonal, on_diagonal, 0.5, None, ALU.mult)
            last.then_inc(w1_ready, 1)
            dve.wait_ge(w1_ready, 1)
            for u in range(U):
                for n in range(2):
                    last = nc.vector.memset(view(diag, u * K, (u + 1) * K, DIAG[n] + u * C0 + NF, [[U * C0, HG]]), 1.0)
            last.then_inc(diag_set, 1)
            nc.vector.memset(view(prod, 0, P, PROD[0] + ONE0, [[2 * P, HG]]), 1.0)

            def v(l, i, j, dims):
                if i >= NS > j:
                    i, j, dims = j, i, [(a, c, b, n) for a, b, c, n in dims]
                start, width = (i * NF + j, NF) if i < NS else (VS + (i - NS) * NC + j - NS, NC)
                return view(V, 0, P, l * VL + start, [[a * VL + b * width + c, n] for a, b, c, n in dims])

            def w(col, row, dims):
                return view(WROW, 0, P, col * P + row, [[a * P + b, n] for a, b, n in dims])

            def columns(lo, hi, first_col, row0, n, f0, symmetric=False):
                for r, i, j, count, d in cyclic_parts(n):
                    out = w(first_col, row0 + r, [(1, 0, hi - lo), (0, 1, count)])
                    direct = v(lo, f0 + i, f0 + j, [(1, 0, 0, hi - lo), (0, 1, 1, count)])
                    if symmetric:
                        add(out, direct, v(f0 + j, f0 + i, lo, [(0, 0, 1, hi - lo), (1, 1, 0, count)]), ALU.add)
                    else:
                        copy(out, direct)

            def columns_rest(lo, hi, first_col, row0, n, f0):
                for r, i, j, count, d in cyclic_parts(n):
                    if d:
                        out = w(first_col, row0 + r, [(1, 0, hi - lo), (0, 1, count)])
                        add(out, out, v(f0 + i, f0 + j, lo, [(0, 0, 1, hi - lo), (1, 1, 0, count)]), ALU.add)

            columns(NF, NF + 1, NF, SS0, NS, S0)
            columns(NF, NF + 1, NF, DD0, ND, D0)
            copy(w(ZX, 0, [(0, NX, ND), (0, 1, NS)]), v(NF, S0, D0, [(0, 0, 1, ND), (0, 1, 0, NS)]))
            copy(w(ZX, NS, [(0, NX, ND), (0, 1, NE)]), v(NF, E0, D0, [(0, 0, 1, ND), (0, 1, 0, NE)]))
            dve.wait_ge(v_saved, NS)
            columns(S0, D0, S0, SS0, NS, S0)
            dve.wait_ge(v_saved, NS + ND)
            columns(D0, E0, D0, DD0, ND, D0)
            columns(S0, D0, S0, DD0, ND, D0, True)

            def finish_weights():
                dve.wait_ge(v_saved, NF)
                dve.wait_ge(small_in, SMALL_IN)
                columns(D0, NF, D0, SS0, NS, S0, True)
                columns(E0, NF, E0, DD0, ND, D0, True)
                copy(w(0, ONE0, [(1, 0, C0)]), view(V, 0, P, VB, [[VL, C0]]))
                add(w(C0, SE0, [(1, 0, ND), (0, NS, NE), (0, 1, NS)]),
                    v(D0, S0, E0, [(1, 0, 0, ND), (0, 0, 1, NE), (0, 1, 0, NS)]),
                    v(E0, S0, D0, [(0, 0, 1, ND), (1, 0, 0, NE), (0, 1, 0, NS)]), ALU.add)
                copy(w(C0 + ND, SE0, [(1, 0, NE + 1), (0, NS, NE), (0, 1, NS)]),
                     v(E0, S0, E0, [(1, 0, 0, NE + 1), (0, 0, 1, NE), (0, 1, 0, NS)]))
                columns(D0, E0, C0, EE0, NE, E0, True)
                columns(E0, NF, C0 + ND, EE0, NE, E0)
                columns(NF, NF + 1, C0 + NC, EE0, NE, E0)
                nc.vector.tensor_scalar(b2k[:, :], b2[:, :], float(K), None, ALU.mult).then_inc(wrow_first, 1)
                dve.wait_ge(wrow_first, 1)
                columns_rest(D0, NF, D0, SS0, NS, S0)
                columns_rest(S0, D0, S0, DD0, ND, D0)
                columns_rest(E0, NF, E0, DD0, ND, D0)
                columns_rest(D0, E0, C0, EE0, NE, E0)
                for e in range(NE):
                    out = w(C0 + ND + e, SE0 + e * NS, [(1, 0, NE - e), (0, 1, NS)])
                    add(out, out, v(S0, E0 + e, E0 + e, [(0, 0, 1, NE - e), (1, 0, 0, NS)]), ALU.add)
                out = w(C0, SE0, [(1, 0, ND), (0, NS, NE), (0, 1, NS)])
                add(out, out, v(S0, E0, D0, [(0, 0, 1, ND), (0, 1, 0, NE), (1, 0, 0, NS)]), ALU.add).then_inc(wrow_ready, 1)

            mul = nc.vector.tensor_tensor

            def products(n, h):
                xt, at = x[n], h * HG

                def p(row, dims):
                    return view(prod, 0, P, PROD[h] + row, dims + [[2 * P, HG]])

                def xs(slot, dims):
                    return view(xt, 0, P, slot * G + at, dims + [[1, HG]])

                for first_row, slot, m in ((SS0, XS, NS), (DD0, XD, ND), (P + EE0, XE, NE)):
                    mul(p(first_row, [[m, m // 2], [1, m]]), xs(slot, [[0, m // 2], [G, m]]),
                        xs(slot, [[G, m // 2], [G, m]]), ALU.mult)
                    mul(p(first_row + m * (m // 2), [[1, m // 2]]), xs(slot, [[G, m // 2]]),
                        xs(slot + m // 2, [[G, m // 2]]), ALU.mult)
                mul(p(P + SE0, [[NS, NE], [1, NS]]), xs(XE, [[G, NE], [0, NS]]), xs(XS, [[0, NE], [G, NS]]), ALU.mult)
                copy(p(P + XS0, [[1, NS]]), xs(XS, [[G, NS]]))
                copy(p(P + XE0, [[1, NE]]), xs(XE, [[G, NE]])).then_inc(prod_ready, 1)

            def transposes(j, n):
                dve.wait_ge(gathered[n], GATHERED * (j + 1))
                for slot, f, m in ((XS, S0, NS), (XS + NS, S0, NS // 2 - 1), (XD, D0, ND), (XD + ND, D0, ND // 2 - 1),
                                   (XE, E0, NE), (XE + NE, E0, NE // 2 - 1)):
                    last = nc.vector.transpose(x[n][:, slot * G:(slot + m) * G], rows[n][:, f * K:(f + m) * K])
                last.then_inc(x_ready, 1)
                dve.wait_ge(x_ready, 2 * j + n + 1)

            def tile(j, n):
                dve.wait_ge(diag_ready, 4 * j + 2 * n - 2)
                transposes(j, n)
                for h in range(2):
                    dve.wait_ge(summed, 8 * j + 4 * n + 2 * h - 2)
                    products(n, h)

            transposes(0, 0)
            products(0, 0)
            finish_weights()
            dve.wait_ge(v_summed, NF)
            nc.vector.memset(view(prod, 0, P, PROD[1] + ONE0, [[2 * P, HG]]), 1.0)
            products(0, 1)
            transposes(0, 1)
            for h in range(2):
                dve.wait_ge(summed, 2 * h + 2)
                products(1, h)
            with dve.Fori(1, NPAIR) as j:
                for n in range(2):
                    tile(j, n)

        @block.scalar
        def _(act):
            for l in range(NF):
                act.wait_ge(v_summed, l + 1)
                nc.scalar.copy(region_a[:, l * VL:(l + 1) * VL], sum_ps[l % 2][:, 0:VL]).then_inc(v_saved, 1)

            def diagonal(n, h):
                for u in range(U):
                    for slot, a, m in ((XS, S0, NS), (XD, D0, ND), (XE, E0, NE)):
                        last = nc.scalar.copy(
                            view(diag, u * K, (u + 1) * K, DIAG[h] + u * C0 + a, [[1, m], [U * C0, HG]]),
                            view(x[n], u * K, (u + 1) * K, slot * G + h * HG, [[G, m], [1, HG]]))
                last.then_inc(diag_ready, 1)

            def save_sums(n, q):
                ps, at = sum_ps[q % 2], SUMS + n * TILE + q * QG * U
                nc.scalar.copy(view(region_a, 0, R0, at, [[PAIR, C0], [QG // 2 * U, 2], [1, QG // 2 * U]]),
                               view(ps, 0, R0, 0, [[1, C0], [BANK, 2], [C0, QG // 2 * U]])).then_inc(sums0_saved, 1)
                nc.scalar.copy(view(region_a, 0, R1, at + C0 * PAIR, [[PAIR, C1], [1, QG * U]]),
                               view(ps, 0, R1, 2 * BANK, [[1, C1], [C1, QG * U]])).then_inc(sums_saved, 1)

            def save_h1(j):
                for m in range(4):
                    if m % 2 == 0:
                        act.wait_ge(h1_summed, 4 * j + m + 2)
                    nc.scalar.activation(h1_sb[:, m * PAIR:(m + 1) * PAIR],
                                         gen[1 - m // 2][:, m % 2 * PAIR:(m % 2 + 1) * PAIR], ACT.Relu,
                                         bias=bt1[:, m:m + 1]).then_inc(h1_saved, 1)

            def save_h2(j):
                act.wait_ge(h2_summed, 2 * j + 2)
                for m in range(2):
                    nc.scalar.activation(h2_sb[:, m * PAIR:(m + 1) * PAIR], gen[1][:, m * PAIR:(m + 1) * PAIR], ACT.Relu,
                                         bias=bt2[:, m:m + 1]).then_inc(h2_saved, 1)

            def save_y(j):
                act.wait_ge(y_summed, j + 1)
                nc.scalar.copy(side[YP:YP + 1, bass.ds(j * PAIR, PAIR)], gen[1][0:1, 0:PAIR]).then_inc(y_saved, 1)

            def pair(j, first=False, last=False):
                for n in range(2):
                    for q in range(4):
                        act.wait_ge(summed, 8 * j + 4 * n + q + 1)
                        save_sums(n, q)
                        if not first and (n, q) == (0, 1):
                            save_h1(j - 1)
                        if not first and (n, q) == (0, 3):
                            save_h2(j - 1)
                        if q % 2 and not n:
                            if q == 1:
                                act.wait_ge(x_ready, 2 * j + 2)
                            diagonal(1, q // 2)
                act.wait_ge(sums_saved, 8 * j + 8)
                for d in range(ND):
                    act.dma_start(cross[d * NX:(d + 1) * NX, :],
                                  region_a[XS0:R1, (C0 + d) * PAIR:(C0 + d + 1) * PAIR]).then_inc(cross_in, 16)
                if not last:
                    act.wait_ge(x_ready, 2 * j + 3)
                    for h in range(2):
                        diagonal(0, h)
                if not first:
                    save_y(j - 1)
                act.wait_ge(z_summed, 2 * j + 2)
                for i in range(2):
                    nc.scalar.activation(z_sb[:, i * PAIR:(i + 1) * PAIR], gen[0][:, i * PAIR:(i + 1) * PAIR],
                                         ACT.Identity, bias=b2k[:, :] if i else 0.0).then_inc(z_saved, 1)

            act.wait_ge(diag_set, 1)
            act.wait_ge(x_ready, 1)
            for h in range(2):
                diagonal(0, h)
            for q in range(NTURN):
                m = min(4, NT - 4 * q)
                act.wait_ge(w_turned, q + 1)
                nc.scalar.copy(weights[:, 4 * q * H:(4 * q + m) * H], gen[q % 2][:, 0:m * H]).then_inc(w_saved, 1)
            pair(0, first=True)
            with act.Fori(1, NPAIR - 1) as j:
                pair(j)
            pair(NPAIR - 1, last=True)
            save_h1(NPAIR - 1)
            save_h2(NPAIR - 1)
            save_y(NPAIR - 1)

        @block.tensor
        def _(pe):
            pe.wait_ge(w2_in, 16)
            pe.wait_ge(w1_ready, 1)
            for l in range(NF):
                if l >= 2:
                    pe.wait_ge(v_saved, l - 1)
                nc.tensor.matmul(sum_ps[l % 2][:, 0:VL], w2_sb[:, l * H:(l + 1) * H], region_a[:, W1S:W1S + VL],
                                 start=True, stop=True).then_inc(v_summed, 1)

            def turn_weights():
                pe.wait_ge(ident_in, 1)
                pe.wait_ge(wrow_ready, 1)
                for q in range(NTURN):
                    if q >= 2:
                        pe.wait_ge(w_saved, q - 1)
                    for c in range(4 * q, min(4 * q + 4, NT)):
                        last = nc.tensor.transpose(gen[q % 2][:, c % 4 * H:(c % 4 + 1) * H], WROW[:, c * P:(c + 1) * P], ident[:, :])
                    last.then_inc(w_turned, 1)

            def sums(n, h, q):
                ps = sum_ps[q % 2]
                for g in range(QG):
                    gh = (q % 2) * QG + g
                    p, d = PROD[h] + gh * 2 * P, DIAG[h] + gh * U * C0
                    o = (g // (QG // 2)) * BANK + g % (QG // 2) * U * C0
                    nc.tensor.matmul(ps[0:R0, o:o + U * C0], prod[:, p:p + R0], diag[:, d:d + U * C0], start=True, stop=True)
                    o = 2 * BANK + g * U * C1
                    last = nc.tensor.matmul(ps[0:R1, o:o + 2 * U * C1], prod[:, p + P:p + P + R1],
                                            view(diag, 0, P, d + D0, [[0, 2], [C0, U], [1, C1]]), start=True, stop=True)
                last.then_inc(summed, 1)

            def weight(block_rows, c):
                return weights[0:block_rows, c * H:(c + 1) * H]

            def saved(block_rows, c):
                return view(region_a, 0, block_rows, SUMS + c * PAIR, [[1, PAIR]])

            def h1(j):
                pe.wait_ge(z_saved, 2 * j + 2)
                for m in range(4):
                    out = gen[1 - m // 2][:, m % 2 * PAIR:(m % 2 + 1) * PAIR]
                    for c in range(2):
                        nc.tensor.matmul(out, wt1[:, c * M1 + m * P:c * M1 + (m + 1) * P], z_sb[:, c * PAIR:(c + 1) * PAIR],
                                         start=c == 0, stop=False)
                    nc.tensor.matmul(out, wt1d[:, m * P:(m + 1) * P], side[0:DN, bass.ds(j * PAIR, PAIR)],
                                     start=False, stop=True).then_inc(h1_summed, 1)

            def h2(j):
                pe.wait_ge(h1_saved, 4 * j + 4)
                for m in range(2):
                    for c in range(4):
                        last = nc.tensor.matmul(gen[1][:, m * PAIR:(m + 1) * PAIR], wt2[:, c * M2 + m * P:c * M2 + (m + 1) * P],
                                                h1_sb[:, c * PAIR:(c + 1) * PAIR], start=c == 0, stop=c == 3)
                    last.then_inc(h2_summed, 1)

            def y(j):
                pe.wait_ge(h2_saved, 2 * j + 2)
                for c in range(2):
                    last = nc.tensor.matmul(gen[1][0:1, 0:PAIR], wt3[:, c:c + 1], h2_sb[:, c * PAIR:(c + 1) * PAIR],
                                            start=c == 0, stop=c == 1)
                last.then_inc(y_summed, 1)

            def quarter(j, n, q):
                if q % 2 == 0:
                    pe.wait_ge(prod_ready, 4 * j + 2 * n + q // 2 + 1)
                    pe.wait_ge(diag_ready, 4 * j + 2 * n + q // 2 + 1)
                sums(n, q // 2, q)

            def z(j):
                z1, z2 = gen[0][:, 0:PAIR], gen[0][:, PAIR:2 * PAIR]
                pe.wait_ge(sums0_saved, 8 * j + 8)
                for a in range(NF):
                    nc.tensor.matmul(z2, weight(R0, a), saved(R0, a), start=a == 0, stop=False)
                pe.wait_ge(sums_saved, 8 * j + 8)
                for a in range(NC):
                    last = nc.tensor.matmul(z2, weight(R1, C0 + a), saved(R1, C0 + a), start=False, stop=a == NC - 1)
                last.then_inc(z_summed, 1)
                nc.tensor.matmul(z1, weight(R0, NF), saved(R0, NF), start=True, stop=False)
                nc.tensor.matmul(z1, weight(R1, C0 + NC), saved(R1, C0 + NC), start=False, stop=False)
                pe.wait_ge(cross_in, CROSS_IN * (j + 1))
                nc.tensor.matmul(z1, weight(RX, ZX), cross[:, :], start=False, stop=True).then_inc(z_summed, 1)

            def pair(j):
                for n in range(2):
                    for q in range(4):
                        pe.wait_ge(sums_saved, 8 * j + 4 * n + q - 1)
                        quarter(j, n, q)
                        if (n, q) == (0, 1):
                            h1(j - 1)
                        if (n, q) == (0, 3):
                            h2(j - 1)
                y(j - 1)
                z(j)

            for n in range(2):
                for q in range(4):
                    if n or q >= 2:
                        pe.wait_ge(sums_saved, 4 * n + q - 1)
                    else:
                        pe.wait_ge(v_saved, NF - 1 + q)
                    quarter(0, n, q)
                    if (n, q) == (0, 1):
                        turn_weights()
            pe.wait_ge(w_saved, NTURN)
            z(0)
            pe.wait_ge(top_in, TOP_IN)
            pe.wait_ge(small_in, SMALL_IN)
            with pe.Fori(1, NPAIR) as j:
                pair(j)
            h1(NPAIR - 1)
            h2(NPAIR - 1)
            y(NPAIR - 1)


def kernel(**inputs):
    import numpy as np
    import concourse.bacc as bacc
    from concourse.bass_utils import run_bass_kernel_spmd

    nc = bacc.Bacc("TRN2", target_bir_lowering=False, num_devices=1)
    a = {name: np.asarray(v) for name, v in inputs.items()}
    a["L0_rec_W2"] = a["L0_rec_W2"].transpose(1, 2, 0)
    a["dense_ctx"] = a["dense_ctx"].reshape(B // TILE, U, G, DN).transpose(3, 0, 2, 1).reshape(DN, B)
    a["b_top1"] = a["b_top1"].reshape(M1 // P, P).T
    a["b_top2"] = a["b_top2"].reshape(M2 // P, P).T
    a["W_top3"] = a["W_top3"].reshape(M2 // P, P).T
    a["L0_rec_b1"] = a["L0_rec_b1"].reshape(H, 1)
    a["L0_rec_b2"] = a["L0_rec_b2"].reshape(H, 1)
    arrays, t = {}, {}
    for name, v in a.items():
        arrays[name] = np.ascontiguousarray(v)
        t[name] = nc.dram_tensor(name, v.shape, mybir.dt.from_np(v.dtype), kind="ExternalInput").ap()
    t["out"] = nc.dram_tensor("out", (1, B), F32, kind="ExternalOutput").ap()
    build(nc, t)
    r = run_bass_kernel_spmd(nc, [arrays], core_ids=[0])
    y = r.results[0]["out"]
    return y.reshape(B // TILE, G, U).transpose(0, 2, 1).reshape(B, 1)
```

```python
from contextlib import ExitStack

import concourse.bass as bass
from concourse import mybir

F32 = mybir.dt.float32
I32 = mybir.dt.int32
ALU = mybir.AluOpType
ACT = mybir.ActivationFunctionType

P = 128

B = 2048
NF = 26
K = 32
H = 128
DN = 16
M1, M2 = 512, 256

NS, ND, NE = 11, 9, 6
S0, E0, D0 = 0, NS, NS + NE
NX = NS + NE
NC = ND + NE


def tri(n):
    return n * (n + 1) // 2


SS0 = 0
DD0 = SS0 + tri(NS)
ONE0 = DD0 + tri(ND)
XD0 = ONE0 + 1
R0 = XD0 + ND
SE0 = 0
EE0 = SE0 + NS * NE
R1 = EE0 + tri(NE)
C0, C1 = NF + 1, NC + 1
NCOL = C0 + C1
XA = P // NX
CROSS = ((0, XA), (XA, ND))
ZX = NCOL
NT = NCOL + 2

U = P // K
TILE = 128
G = TILE // U
HG = G // 2
QG = HG // 2
NTILE = B // TILE
NPAIR = NTILE // 2
BANK = 512

XS, XD = 0, NS + (NS - 1) // 2
XE = XD + ND + (ND - 1) // 2
SLOTS = XE + NE + (NE - 1) // 2

VE = NS * NF
VD = VE + NE * NC
VB = VD + ND * ND
VL = VB + 1
assert VL <= BANK


def cyclic_parts(n):
    for d in range(n // 2 + 1):
        last = n // 2 if 2 * d == n else n
        unwrapped = min(n - d, last)
        yield d * n, 0, d, unwrapped, d
        if last > unwrapped:
            yield d * n + unwrapped, unwrapped, 0, last - unwrapped, d


def view(tensor, p0, p1, offset, dims):
    base = tensor[p0:p1, offset:offset + 1]
    return bass.AP(base.tensor, base.offset, [list(base.ap[0])] + [list(d) for d in dims])


def build(nc, t):
    with ExitStack() as ctx:
        def sb(name, shape, dt=F32):
            return ctx.enter_context(nc.sbuf_tensor(name, shape, dt))

        def pb(name, n):
            return ctx.enter_context(nc.psum_tensor(name, [P, n * BANK], F32))

        def sem(name):
            return ctx.enter_context(nc.semaphore(name))

        region_a = sb("region_a", [P, max((NF + 1) * VL, 2 * NCOL * TILE)])
        V = region_a
        W1S = NF * VL
        SUMS = [0, NCOL * TILE]
        NPROD = HG * 2 * P
        prod = sb("prod", [P, 2 * NPROD])
        PROD = [0, NPROD]
        w2_sb = prod[:, NPROD:NPROD + NF * H]
        W1_RAW = NPROD + NF * H
        diag = sb("diag", [P, G * U * C0])
        TOPW = 8 * TILE
        region_b = sb("region_b", [P, max(NT * P, TOPW + 3 * M1 + 4 * M2)])
        WROW = region_b
        z_sb = region_b[:, 0:2 * TILE]
        h1_sb = region_b[:, 2 * TILE:6 * TILE]
        h2_sb = region_b[:, 6 * TILE:8 * TILE]
        wt1 = region_b[:, TOPW:TOPW + 2 * M1]
        wt1d = region_b[0:DN, TOPW + 2 * M1:TOPW + 3 * M1]
        wt2 = region_b[:, TOPW + 3 * M1:TOPW + 3 * M1 + 4 * M2]
        weights = sb("weights", [P, NT * H])
        index = [sb(f"index{n}", [P, NF], I32) for n in range(2)]
        rows = [sb(f"rows{n}", [P, NF * K]) for n in range(2)]
        x = [sb(f"x{n}", [P, SLOTS * G]) for n in range(2)]
        wt3 = sb("wt3", [P, 2])
        bt1 = sb("bt1", [P, 4])
        bt2 = sb("bt2", [P, 2])
        b2 = sb("b2", [P, 1])
        b2k = sb("b2k", [P, 1])
        ident = sb("ident", [P, P])
        cross = [sb(f"cross{i}", [(hi - lo) * NX, 2 * TILE]) for i, (lo, hi) in enumerate(CROSS)]
        side = sb("side", [64, B])
        YP = 32

        sum_ps = [pb(f"sum_ps{n}", 3) for n in range(2)]
        gen = [pb(f"gen{n}", 1) for n in range(2)]

        index_in = [sem(f"index_in{n}") for n in range(2)]
        gathered_se = [sem(f"gathered_se{n}") for n in range(2)]
        gathered_d = [sem(f"gathered_d{n}") for n in range(2)]
        w1_in, w2_in, ident_in = sem("w1_in"), sem("w2_in"), sem("ident_in")
        small_in, top_in = sem("small_in"), sem("top_in")
        turns = sem("turns")
        ident0 = sem("ident0")
        w1_sum, w1_ready = sem("w1_sum"), sem("w1_ready")
        v_summed, v_saved = sem("v_summed"), sem("v_saved")
        wrow_first, wrow_ready = sem("wrow_first"), sem("wrow_ready")
        wrow0_ready = sem("wrow0_ready")
        w_turned, w_saved = sem("w_turned"), sem("w_saved")
        diag_set = sem("diag_set")
        x_se_ready = [sem(f"x_se_ready{n}") for n in range(2)]
        x_d_ready = [sem(f"x_d_ready{n}") for n in range(2)]
        prod_ready = sem("prod_ready")
        diag_ready = sem("diag_ready")
        summed = sem("summed")
        sums_saved = sem("sums_saved")
        sums0_saved = [sem(f"sums0_saved{n}") for n in range(2)]
        cross_in = sem("cross_in")
        z_summed, z_saved = sem("z_summed"), sem("z_saved")
        h1_summed, h1_saved = sem("h1_summed"), sem("h1_saved")
        h2_summed, h2_saved = sem("h2_summed"), sem("h2_saved")
        y_summed, y_saved, y_out = sem("y_summed"), sem("y_saved"), sem("y_out")

        GATHERED_SE, GATHERED_D = 16 * NX, 16 * ND
        CROSS_IN = 16 * len(CROSS)
        SMALL_IN = 16 * 5
        TOP_IN = 16 * 3

        NTURN = -(-NT // 4)
        NTURN0 = C0 // 4

        block = ctx.enter_context(nc.Block())

        @block.sync
        def _(sp):
            for n in range(2):
                sp.dma_start(index[n][:, :], t["ids"][n * TILE:(n + 1) * TILE, :]).then_inc(index_in[n], 16)
            sp.dma_start(prod[:, W1_RAW:W1_RAW + NF * NF], t["L0_rec_W1"].rearrange("h i j -> h (i j)")).then_inc(w1_in, 16)
            sp.dma_start(region_a[:, W1S + VB:W1S + VB + 1], t["L0_rec_b1"]).then_inc(w1_in, 16)
            sp.dma_start(w2_sb, t["L0_rec_W2"].rearrange("i l h -> i (l h)")).then_inc(w2_in, 16)
            sp.dma_start(wt3[:, :], t["W_top3"]).then_inc(small_in, 16)
            sp.dma_start(bt1[:, :], t["b_top1"]).then_inc(small_in, 16)
            sp.dma_start(bt2[:, :], t["b_top2"]).then_inc(small_in, 16)
            sp.dma_start(b2[:, :], t["L0_rec_b2"]).then_inc(small_in, 16)
            sp.dma_start(side[0:DN, :], t["dense_ctx"]).then_inc(small_in, 16)

            def lay_cross(pairs, n):
                sp.wait_ge(sums0_saved[n], 4 * pairs)
                for rows_of, (lo, hi) in zip(cross, CROSS):
                    sp.dma_start(rows_of[:, n * TILE:(n + 1) * TILE],
                                 view(region_a, XD0 + lo, XD0 + hi, SUMS[n], [[TILE, NX], [1, TILE]])).then_inc(cross_in, 16)

            with sp.Fori(1, NPAIR) as j:
                for n in range(2):
                    sp.wait_ge(x_d_ready[n], j)
                    sp.dma_start(index[n][:, :], t["ids"][bass.ds(j * 2 * TILE + n * TILE, TILE), :]).then_inc(index_in[n], 16)
                    lay_cross(j, n)
            for n in range(2):
                lay_cross(NPAIR, n)
            sp.wait_ge(y_saved, NTILE)
            sp.dma_start(t["out"], side[YP:YP + 1, :]).then_inc(y_out, 16)
            sp.wait_ge(y_out, 16)

        @block.gpsimd
        def _(pool):
            def gather(j, n, first):
                pool.wait_ge(index_in[n], 16 * (j + 1))
                if not first:
                    pool.wait_ge(x_d_ready[n], j)
                    pool.sem_inc(turns, 1)
                for f in range(NF):
                    pool.indirect_dma_start(
                        out=rows[n][:, f * K:(f + 1) * K], out_offset=None, in_=t[f"tbl_{f}"],
                        in_offset=bass.IndirectOffsetOnAxis(ap=index[n][:, f:f + 1], axis=0),
                    ).then_inc(gathered_d[n] if f >= D0 else gathered_se[n], 16)

            nc.gpsimd.memset(ident[:, :], 0.0).then_inc(ident0, 1)
            pool.wait_ge(ident0, 1)
            nc.gpsimd.affine_select(out=ident[:, :], in_=ident[:, :], compare_op=ALU.not_equal, fill=1.0, base=0,
                                    pattern=[[-1, P]], channel_multiplier=1).then_inc(ident_in, 1)
            gather(0, 0, True)
            gather(0, 1, True)
            with pool.Fori(1, NPAIR) as j:
                for n in range(2):
                    gather(j, n, False)

        @block.vector
        def _(dve):
            add, copy = nc.vector.tensor_tensor, nc.vector.tensor_copy
            nc.vector.memset(diag[:, :], 0.0)
            nc.vector.memset(WROW[:, C0 * P:NT * P], 0.0)
            nc.vector.memset(view(WROW, 0, P, ONE0, [[P, C0], [1, P - ONE0]]), 0.0)
            dve.wait_ge(w1_in, 32)
            for at, f0, m, width in ((0, S0, NS, NF), (VE, E0, NE, NC), (VD, D0, ND, ND)):
                corner = W1_RAW + f0 * NF + f0
                last = add(view(V, 0, P, W1S + at, [[width, m], [1, width]]),
                           view(prod, 0, P, corner, [[NF, m], [1, width]]),
                           view(prod, 0, P, corner, [[1, m], [NF, width]]), ALU.add)
            last.then_inc(w1_sum, 1)
            dve.wait_ge(w1_sum, 1)
            for at, m, width in ((0, NS, NF), (VE, NE, NC), (VD, ND, ND)):
                on_diagonal = view(V, 0, P, W1S + at, [[width + 1, m]])
                last = nc.vector.tensor_scalar(on_diagonal, on_diagonal, 0.5, None, ALU.mult)
            last.then_inc(w1_ready, 1)
            dve.wait_ge(w1_ready, 1)
            for u in range(U):
                last = nc.vector.memset(view(diag, u * K, (u + 1) * K, u * C0 + NF, [[U * C0, G]]), 1.0)
            last.then_inc(diag_set, 1)
            nc.vector.memset(view(prod, 0, P, PROD[0] + ONE0, [[2 * P, HG]]), 1.0)

            def v(l, i, j, dims):
                if i >= NS > j or i >= D0 > j:
                    i, j, dims = j, i, [(a, c, b, n) for a, b, c, n in dims]
                at, f0, width = (0, 0, NF) if i < NS else (VE, E0, NC) if i < D0 else (VD, D0, ND)
                start = at + (i - f0) * width + j - f0
                return view(V, 0, P, l * VL + start, [[a * VL + b * width + c, n] for a, b, c, n in dims])

            def w(col, row, dims):
                return view(WROW, 0, P, col * P + row, [[a * P + b, n] for a, b, n in dims])

            def columns(lo, hi, first_col, row0, n, f0, symmetric=False):
                for r, i, j, count, d in cyclic_parts(n):
                    out = w(first_col, row0 + r, [(1, 0, hi - lo), (0, 1, count)])
                    direct = v(lo, f0 + i, f0 + j, [(1, 0, 0, hi - lo), (0, 1, 1, count)])
                    if symmetric:
                        last = add(out, direct, v(f0 + j, f0 + i, lo, [(0, 0, 1, hi - lo), (1, 1, 0, count)]), ALU.add)
                    else:
                        last = copy(out, direct)
                return last

            def columns_rest(lo, hi, first_col, row0, n, f0):
                for r, i, j, count, d in cyclic_parts(n):
                    if d:
                        out = w(first_col, row0 + r, [(1, 0, hi - lo), (0, 1, count)])
                        last = add(out, out, v(f0 + i, f0 + j, lo, [(0, 0, 1, hi - lo), (1, 1, 0, count)]), ALU.add)
                return last

            mul = nc.vector.tensor_tensor

            def transposes(n, sets):
                for slot, f, m in sets:
                    nc.vector.transpose(x[n][:, slot * G:(slot + m) * G], rows[n][:, f * K:(f + m) * K])
                    head = (m - 1) // 2
                    last = nc.vector.transpose(x[n][:, (slot + m) * G:(slot + m + head) * G], rows[n][:, f * K:(f + head) * K])
                return last

            def products(n, h, halves, sets):
                g, at = halves * HG, h * HG

                def p(row, dims):
                    return view(prod, 0, P, PROD[h] + row, dims + [[2 * P, g]])

                def xs(slot, dims):
                    return view(x[n], 0, P, slot * G + at, dims + [[1, g]])

                for first_row, slot, m in sets:
                    shifts = (m + 1) // 2
                    last = mul(p(first_row, [[m, shifts], [1, m]]), xs(slot, [[0, shifts], [G, m]]),
                               xs(slot, [[G, shifts], [G, m]]), ALU.mult)
                    if m % 2 == 0:
                        last = mul(p(first_row + m * shifts, [[1, m // 2]]), xs(slot, [[G, m // 2]]),
                                   xs(slot + m // 2, [[G, m // 2]]), ALU.mult)
                if len(sets) == 2:
                    last = mul(p(P + SE0, [[NS, NE], [1, NS]]), xs(XE, [[G, NE], [0, NS]]), xs(XS, [[0, NE], [G, NS]]), ALU.mult)
                else:
                    last = copy(p(XD0, [[1, ND]]), xs(XD, [[G, ND]]))
                return last

            SE_FIELDS, D_FIELDS = ((XS, S0, NS), (XE, E0, NE)), ((XD, D0, ND),)
            SE_PAIRS, D_PAIRS = ((SS0, XS, NS), (P + EE0, XE, NE)), ((DD0, XD, ND),)

            def x_se(j, n):
                dve.wait_ge(gathered_se[n], GATHERED_SE * (j + 1))
                transposes(n, SE_FIELDS).then_inc(x_se_ready[n], 1)
                dve.wait_ge(x_se_ready[n], j + 1)

            def x_d(j, n):
                dve.wait_ge(gathered_d[n], GATHERED_D * (j + 1))
                transposes(n, D_FIELDS).then_inc(x_d_ready[n], 1)
                dve.wait_ge(x_d_ready[n], j + 1)

            def tile(j, n):
                x_se(j, n)
                dve.wait_ge(summed, 4 * (2 * j + n))
                products(n, 0, 2, SE_PAIRS)
                x_d(j, n)
                for h in range(2):
                    products(n, h, 1, D_PAIRS).then_inc(prod_ready, 1)

            columns(NF, NF + 1, NF, SS0, NS, S0)
            columns(NF, NF + 1, NF, DD0, ND, D0)
            columns(NF, NF + 1, C0 + NC, EE0, NE, E0)
            for i, (lo, hi) in enumerate(CROSS):
                for f0, m in ((S0, NS), (E0, NE)):
                    copy(w(ZX + i, f0, [(0, NX, hi - lo), (0, 1, m)]), v(NF, D0 + lo, f0, [(0, 1, 0, hi - lo), (0, 0, 1, m)]))
            dve.wait_ge(v_saved, NS)
            columns(S0, E0, S0, SS0, NS, S0)
            x_se(0, 0)
            products(0, 0, 1, SE_PAIRS)
            dve.wait_ge(v_saved, NX)
            columns(E0, D0, E0, SS0, NS, S0, True)
            for lo, m, col in ((E0, NE, C0), (NF, 1, C0 + NC)):
                copy(w(col, SE0, [(1, 0, m), (0, NS, NE), (0, 1, NS)]), v(lo, S0, E0, [(1, 0, 0, m), (0, 0, 1, NE), (0, 1, 0, NS)]))
            columns(E0, D0, C0, EE0, NE, E0).then_inc(wrow_first, 1)
            dve.wait_ge(wrow_first, 1)
            columns_rest(E0, D0, E0, SS0, NS, S0)
            for e in range(NE):
                out = w(C0 + e, SE0 + e * NS, [(1, 0, NE - e), (0, 1, NS)])
                add(out, out, v(S0, E0 + e, E0 + e, [(0, 0, 1, NE - e), (1, 0, 0, NS)]), ALU.add)
            x_d(0, 0)
            products(0, 0, 1, D_PAIRS).then_inc(prod_ready, 1)

            def finish_block0():
                columns(D0, NF, D0, SS0, NS, S0, True)
                columns(D0, NF, D0, DD0, ND, D0)
                columns(S0, E0, S0, DD0, ND, D0, True)
                columns(E0, D0, E0, DD0, ND, D0, True)
                copy(w(0, ONE0, [(1, 0, C0)]), view(V, 0, P, VB, [[VL, C0]])).then_inc(wrow_first, 1)
                dve.wait_ge(wrow_first, 2)
                columns_rest(D0, NF, D0, SS0, NS, S0)
                columns_rest(S0, E0, S0, DD0, ND, D0)
                columns_rest(E0, D0, E0, DD0, ND, D0).then_inc(wrow0_ready, 1)

            def finish_block1():
                across = w(C0 + NE, SE0, [(1, 0, ND), (0, NS, NE), (0, 1, NS)])
                add(across, v(D0, S0, E0, [(1, 0, 0, ND), (0, 0, 1, NE), (0, 1, 0, NS)]),
                    v(E0, S0, D0, [(0, 0, 1, ND), (1, 0, 0, NE), (0, 1, 0, NS)]), ALU.add)
                columns(D0, NF, C0 + NE, EE0, NE, E0, True).then_inc(wrow_first, 1)
                dve.wait_ge(wrow_first, 3)
                columns_rest(D0, NF, C0 + NE, EE0, NE, E0)
                add(across, across, v(S0, E0, D0, [(0, 0, 1, ND), (0, 1, 0, NE), (1, 0, 0, NS)]), ALU.add).then_inc(wrow_ready, 1)

            dve.wait_ge(v_saved, NF)
            finish_block0()
            finish_block1()
            dve.wait_ge(small_in, SMALL_IN)
            nc.vector.tensor_scalar(b2k[:, :], b2[:, :], float(K), None, ALU.mult)
            dve.wait_ge(v_summed, NF)
            nc.vector.memset(view(prod, 0, P, PROD[1] + ONE0, [[2 * P, HG]]), 1.0)
            products(0, 1, 1, SE_PAIRS)
            products(0, 1, 1, D_PAIRS).then_inc(prod_ready, 1)
            tile(0, 1)
            with dve.Fori(1, NPAIR) as j:
                for n in range(2):
                    dve.wait_ge(diag_ready, 2 * j + n - 1)
                    tile(j, n)

        @block.scalar
        def _(act):
            SE_SETS, D_SETS = ((XS, S0, NS), (XE, E0, NE)), ((XD, D0, ND),)

            def spread(n, slot, a, m, u):
                return nc.scalar.copy(view(diag, u * K, (u + 1) * K, u * C0 + a, [[1, m], [U * C0, G]]),
                                      view(x[n], u * K, (u + 1) * K, slot * G, [[G, m], [1, G]]))

            def diagonal(j, n):
                for ready, sets in ((x_se_ready[n], SE_SETS), (x_d_ready[n], D_SETS)):
                    act.wait_ge(ready, j + 1)
                    for slot, a, m in sets:
                        for u in range(U):
                            last = spread(n, slot, a, m, u)
                last.then_inc(diag_ready, 1)

            def save_sums(n, q):
                ps, at = sum_ps[q % 2], SUMS[n] + q * QG * U
                nc.scalar.copy(view(region_a, 0, R0, at, [[TILE, C0], [QG // 2 * U, 2], [1, QG // 2 * U]]),
                               view(ps, 0, R0, 0, [[1, C0], [BANK, 2], [C0, QG // 2 * U]])).then_inc(sums0_saved[n], 1)
                nc.scalar.copy(view(region_a, 0, R1, at + C0 * TILE, [[TILE, C1], [1, QG * U]]),
                               view(ps, 0, R1, 2 * BANK, [[1, C1], [C1, QG * U]])).then_inc(sums_saved, 1)

            def save_z(t):
                act.wait_ge(z_summed, 2 * t + 2)
                for i in range(2):
                    nc.scalar.activation(z_sb[:, i * TILE:(i + 1) * TILE], gen[0][:, i * TILE:(i + 1) * TILE],
                                         ACT.Identity, bias=b2k[:, :] if i else 0.0).then_inc(z_saved, 1)

            def save_h1(t):
                for m in range(4):
                    if m % 2 == 0:
                        act.wait_ge(h1_summed, 4 * t + m + 2)
                    nc.scalar.activation(h1_sb[:, m * TILE:(m + 1) * TILE], gen[1 - m // 2][:, m % 2 * TILE:(m % 2 + 1) * TILE],
                                         ACT.Relu, bias=bt1[:, m:m + 1]).then_inc(h1_saved, 1)

            def save_h2(t):
                act.wait_ge(h2_summed, 2 * t + 2)
                for m in range(2):
                    nc.scalar.activation(h2_sb[:, m * TILE:(m + 1) * TILE], gen[1][:, m * TILE:(m + 1) * TILE], ACT.Relu,
                                         bias=bt2[:, m:m + 1]).then_inc(h2_saved, 1)

            def save_y(t):
                act.wait_ge(y_summed, t + 1)
                nc.scalar.copy(side[YP:YP + 1, bass.ds(t * TILE, TILE)], gen[1][0:1, 0:TILE]).then_inc(y_saved, 1)

            def tile(j, n):
                t = 2 * j + n
                diagonal(j, n)
                save_z(t - 1)
                for q in range(4):
                    act.wait_ge(summed, 4 * t + q + 1)
                    save_sums(n, q)
                    if q == 1:
                        save_h1(t - 1)
                save_h2(t - 1)
                save_y(t - 1)

            act.wait_ge(diag_set, 1)
            SE_AT = NS + 3
            for l in range(NF):
                act.wait_ge(v_summed, l + 1)
                nc.scalar.copy(region_a[:, l * VL:(l + 1) * VL], sum_ps[l % 2][:, 0:VL]).then_inc(v_saved, 1)
                if l == SE_AT:
                    act.wait_ge(x_se_ready[0], 1)
                if SE_AT <= l < SE_AT + 2 * U:
                    spread(0, *SE_SETS[(l - SE_AT) // U], (l - SE_AT) % U)
            act.wait_ge(x_d_ready[0], 1)
            for u in range(U):
                last = spread(0, *D_SETS[0], u)
            last.then_inc(diag_ready, 1)

            def save_weights(first, end):
                for q in range(first, end):
                    m = min(4, NT - 4 * q)
                    act.wait_ge(w_turned, q + 1)
                    nc.scalar.copy(weights[:, 4 * q * H:(4 * q + m) * H], gen[q % 2][:, 0:m * H]).then_inc(w_saved, 1)

            def save_first(q):
                act.wait_ge(summed, q + 1)
                save_sums(0, q)

            save_weights(0, NTURN0)
            act.wait_ge(wrow_ready, 1)
            save_first(0)
            save_weights(NTURN0, NTURN0 + 2)
            save_first(1)
            save_weights(NTURN0 + 2, NTURN - 3)
            save_first(2)
            save_weights(NTURN - 3, NTURN - 1)
            save_first(3)
            save_weights(NTURN - 1, NTURN)
            act.dma_start(wt1, t["W_top1"][0:2 * H, :].rearrange("(c p) n -> p c n", p=P)).then_inc(top_in, 16)
            act.dma_start(wt1d, t["W_top1"][2 * H:2 * H + DN, :]).then_inc(top_in, 16)
            act.dma_start(wt2, t["W_top2"].rearrange("(c p) n -> p c n", p=P)).then_inc(top_in, 16)
            tile(0, 1)
            with act.Fori(1, NPAIR) as j:
                for n in range(2):
                    tile(j, n)
            save_z(NTILE - 1)
            save_h1(NTILE - 1)
            save_h2(NTILE - 1)
            save_y(NTILE - 1)

        @block.tensor
        def _(pe):
            pe.wait_ge(w2_in, 16)
            pe.wait_ge(w1_ready, 1)
            for l in range(NF):
                if l >= 2:
                    pe.wait_ge(v_saved, l - 1)
                nc.tensor.matmul(sum_ps[l % 2][:, 0:VL], w2_sb[:, l * H:(l + 1) * H], region_a[:, W1S:W1S + VL],
                                 start=True, stop=True).then_inc(v_summed, 1)

            def turn_weights(first, end):
                for q in range(first, end):
                    if q == NTURN0:
                        pe.wait_ge(wrow_ready, 1)
                    if q >= 2:
                        pe.wait_ge(w_saved, q - 1)
                    for c in range(4 * q, min(4 * q + 4, NT)):
                        last = nc.tensor.transpose(gen[q % 2][:, c % 4 * H:(c % 4 + 1) * H], WROW[:, c * P:(c + 1) * P], ident[:, :])
                    last.then_inc(w_turned, 1)

            def sums(q):
                ps = sum_ps[q % 2]
                for g in range(QG):
                    g_tile = q * QG + g
                    p, d = g_tile * 2 * P, g_tile * U * C0
                    o = (g // (QG // 2)) * BANK + g % (QG // 2) * U * C0
                    nc.tensor.matmul(ps[0:R0, o:o + U * C0], prod[:, p:p + R0], diag[:, d:d + U * C0], start=True, stop=True)
                    o = 2 * BANK + g * U * C1
                    last = nc.tensor.matmul(ps[0:R1, o:o + U * C1], prod[:, p + P:p + P + R1],
                                            view(diag, 0, P, d + NS, [[C0, U], [1, C1]]), start=True, stop=True)
                last.then_inc(summed, 1)

            def weight(block_rows, c):
                return weights[0:block_rows, c * H:(c + 1) * H]

            def h1(t):
                def out(m):
                    return gen[1 - m // 2][:, m % 2 * TILE:(m % 2 + 1) * TILE]

                def z_term(m, c):
                    return nc.tensor.matmul(out(m), wt1[:, c * M1 + m * P:c * M1 + (m + 1) * P],
                                            z_sb[:, c * TILE:(c + 1) * TILE],
                                            start=c == 0 and m % 2 == 0, stop=c == 1 and m % 2 == 1)

                for half in range(2):
                    if half == 0:
                        pe.wait_ge(z_saved, 2 * t + 1)
                    for m in (2 * half, 2 * half + 1):
                        z_term(m, 0)
                        nc.tensor.matmul(out(m), wt1d[:, m * P:(m + 1) * P], side[0:DN, bass.ds(t * TILE, TILE)],
                                         start=False, stop=False)
                    if half == 0:
                        pe.wait_ge(z_saved, 2 * t + 2)
                    for m in (2 * half, 2 * half + 1):
                        z_term(m, 1).then_inc(h1_summed, 1)

            def h2(t):
                for half in range(2):
                    pe.wait_ge(h1_saved, 4 * t + 2 * half + 2)
                    for m in range(2):
                        for c in (2 * half, 2 * half + 1):
                            last = nc.tensor.matmul(gen[1][:, m * TILE:(m + 1) * TILE],
                                                    wt2[:, c * M2 + m * P:c * M2 + (m + 1) * P],
                                                    h1_sb[:, c * TILE:(c + 1) * TILE],
                                                    start=c == 0 and m == 0, stop=c == 3 and m == 1)
                        if half:
                            last.then_inc(h2_summed, 1)

            def y(t):
                pe.wait_ge(h2_saved, 2 * t + 2)
                for c in range(2):
                    last = nc.tensor.matmul(gen[1][0:1, 0:TILE], wt3[:, c:c + 1], h2_sb[:, c * TILE:(c + 1) * TILE],
                                            start=c == 0, stop=c == 1)
                last.then_inc(y_summed, 1)

            def z(j, n, first=False):
                z1, z2 = gen[0][:, 0:TILE], gen[0][:, TILE:2 * TILE]

                def term(out, block_rows, c, values, start=False, stop=False):
                    return nc.tensor.matmul(out, weights[0:block_rows, c * H:(c + 1) * H], values, start=start, stop=stop)

                def saved(block_rows, c):
                    return region_a[0:block_rows, SUMS[n] + c * TILE:SUMS[n] + (c + 1) * TILE]

                pe.wait_ge(sums0_saved[n], 4 * (j + 1))
                for a in range(NF):
                    term(z2, R0, a, saved(R0, a), start=a == 0)
                    if a == NS and not first:
                        y(2 * j + n - 1)
                pe.wait_ge(sums_saved, 4 * (2 * j + n) + 4)
                if first:
                    pe.wait_ge(w_saved, NTURN)
                for a in range(NC):
                    end = term(z2, R1, C0 + a, saved(R1, C0 + a), stop=a == NC - 1)
                end.then_inc(z_summed, 1)
                term(z1, R0, NF, saved(R0, NF), start=True)
                term(z1, R1, C0 + NC, saved(R1, C0 + NC))
                pe.wait_ge(cross_in, CROSS_IN * (2 * j + n + 1))
                for i, (lo, hi) in enumerate(CROSS):
                    end = term(z1, (hi - lo) * NX, ZX + i, cross[i][:, n * TILE:(n + 1) * TILE], stop=i == len(CROSS) - 1)
                end.then_inc(z_summed, 1)

            def tile(j, n):
                t = 2 * j + n
                for q in range(4):
                    pe.wait_ge(sums_saved, 4 * t + q - 1)
                    if q == 0:
                        pe.wait_ge(diag_ready, t + 1)
                    if q % 2 == 0:
                        pe.wait_ge(prod_ready, 2 * t + q // 2 + 1)
                    sums(q)
                    if q == 1:
                        h1(t - 1)
                h2(t - 1)
                z(j, n)

            pe.wait_ge(diag_ready, 1)
            pe.wait_ge(prod_ready, 1)
            for q in range(2):
                pe.wait_ge(v_saved, NF - 1 + q)
                sums(q)
            pe.wait_ge(ident_in, 1)
            pe.wait_ge(wrow0_ready, 1)
            turn_weights(0, NTURN - 3)
            pe.wait_ge(prod_ready, 2)
            for q in range(2, 4):
                pe.wait_ge(sums_saved, q - 1)
                sums(q)
                if q == 2:
                    turn_weights(NTURN - 3, NTURN - 1)
            turn_weights(NTURN - 1, NTURN)
            pe.wait_ge(w_saved, NTURN - 1)
            z(0, 0, first=True)
            pe.wait_ge(top_in, TOP_IN)
            pe.wait_ge(small_in, SMALL_IN)
            tile(0, 1)
            with pe.Fori(1, NPAIR) as j:
                for n in range(2):
                    tile(j, n)
            h1(NTILE - 1)
            h2(NTILE - 1)
            y(NTILE - 1)


def kernel(**inputs):
    import numpy as np
    import concourse.bacc as bacc
    from concourse.bass_utils import run_bass_kernel_spmd

    nc = bacc.Bacc("TRN2", target_bir_lowering=False, num_devices=1)
    a = {name: np.asarray(v) for name, v in inputs.items()}
    a["L0_rec_W2"] = a["L0_rec_W2"].transpose(1, 2, 0)
    a["dense_ctx"] = a["dense_ctx"].reshape(B // TILE, U, G, DN).transpose(3, 0, 2, 1).reshape(DN, B)
    a["b_top1"] = a["b_top1"].reshape(M1 // P, P).T
    a["b_top2"] = a["b_top2"].reshape(M2 // P, P).T
    a["W_top3"] = a["W_top3"].reshape(M2 // P, P).T
    a["L0_rec_b1"] = a["L0_rec_b1"].reshape(H, 1)
    a["L0_rec_b2"] = a["L0_rec_b2"].reshape(H, 1)
    arrays, t = {}, {}
    for name, v in a.items():
        arrays[name] = np.ascontiguousarray(v)
        t[name] = nc.dram_tensor(name, v.shape, mybir.dt.from_np(v.dtype), kind="ExternalInput").ap()
    t["out"] = nc.dram_tensor("out", (1, B), F32, kind="ExternalOutput").ap()
    build(nc, t)
    r = run_bass_kernel_spmd(nc, [arrays], core_ids=[0])
    y = r.results[0]["out"]
    return y.reshape(B // TILE, G, U).transpose(0, 2, 1).reshape(B, 1)
```
